# Optimizing a Trainium2 kernel written in Bass

```python
import numpy as np
import jax
import jax.numpy as jnp

def _softmax(x, axis=-1):
    return jax.nn.softmax(x, axis=axis)

def _gelu(x):
    return jax.nn.gelu(x, approximate=True)

def _silu(x):
    return jax.nn.silu(x)

def _sigmoid(x):
    return jax.nn.sigmoid(x)

def _layernorm(x, axis=-1, eps=1e-05):
    m = jnp.mean(x, axis=axis, keepdims=True)
    v = jnp.var(x, axis=axis, keepdims=True)
    return (x - m) / jnp.sqrt(v + eps)

def _scatter_add(tgt, idx, src, axis=0):
    return tgt.at[idx].add(src)

def _segment_sum(src, seg, n):
    return jax.ops.segment_sum(src, seg, n)
kernel_name = 'mk_adaln_ffn_d1_seqx_r4_ec64cc'

def setup_inputs(seed: int=0):
    np.random.seed(seed)
    _w = jnp.asarray

    def _rec_inputs():
        import jax
        import jax.numpy as jnp
        _rk = jax.random.key(seed)
        x = -0.000125 + 0.9999 * jax.random.normal(jax.random.fold_in(_rk, 1), (64, 64, 1024), jnp.float32)
        _lenS = 64 - jax.random.randint(jax.random.fold_in(_rk, 7), (64,), 0, max(1, 64 // 4) + 1, jnp.int32)
        _lenS2 = 64 - jax.random.randint(jax.random.fold_in(_rk, 8), (64,), 0, max(1, 64 // 4) + 1, jnp.int32)
        cond_128 = 0.0061147 + 1.02565 * jax.random.normal(jax.random.fold_in(_rk, 11), (64, 128), jnp.float32)
        fside_S_0 = -0.022604 + 0.987366 * jax.random.normal(jax.random.fold_in(_rk, 12), (64,), jnp.float32)
        return (x, cond_128, fside_S_0)
    x, cond_128, fside_S_0 = _rec_inputs()

    def _L0_cond_setup():
        import jax, jax.numpy as jnp
        import numpy as np
        from jax import lax
        N, C_IN, L = (32, 64, 1024)
        C_OUT, K, GROUPS = (64, 9, 4)
        C_DIM, PAD, STRIDE = (128, 4, 1)
        key = jax.random.key(seed)
        k1, k2, k3, k4, k5 = jax.random.split(key, 5)
        x = jax.random.normal(k1, (N, C_IN, L), dtype=jnp.float32)
        c = jax.random.normal(k2, (N, C_DIM), dtype=jnp.float32)
        weight = jax.random.normal(k3, (C_OUT, C_IN // GROUPS, K), dtype=jnp.float32)
        c_weight = jax.random.normal(k4, (C_OUT, C_DIM), dtype=jnp.float32)
        bias = jax.random.normal(k5, (C_OUT,), dtype=jnp.float32)
        return {'x': x, 'c': c, 'weight': weight, 'c_weight': c_weight, 'bias': bias}
    _L0_cond_all = _L0_cond_setup()
    _L0_cond_in = {k: v for k, v in _L0_cond_all.items() if k in ('weight', 'c_weight')}
    del _L0_cond_all

    def _L0_ffn_setup():
        import jax, jax.numpy as jnp
        import numpy as np
        B, S, D = (4, 512, 1024)
        NUM_EXPERTS, TOP_K = (3, 2)

        def _expert_outputs(h, w1, b1, w2, b2):
            pre = jnp.einsum('bsd,edf->ebsf', h, w1) + b1[:, None, None, :]
            act = jnp.stack([jnp.tanh(pre[0]), jax.nn.gelu(pre[1], approximate=False), jax.nn.silu(pre[2])])
            return jnp.einsum('ebsf,efd->ebsd', act, w2) + b2[:, None, None, :]
        key = jax.random.key(seed)
        ks = jax.random.split(key, 8)
        scale_in = 1.0 / np.sqrt(D)
        scale_gate = 1.0 / np.sqrt(D + 1)
        return {'h': jax.random.normal(ks[0], (B, S, D), dtype=jnp.float32), 'gate_w': jax.random.uniform(ks[1], (D + 1, NUM_EXPERTS), minval=-scale_gate, maxval=scale_gate, dtype=jnp.float32), 'gate_b': jnp.zeros((NUM_EXPERTS,), dtype=jnp.float32), 'w1': jax.random.uniform(ks[2], (NUM_EXPERTS, D, D), minval=-scale_in, maxval=scale_in, dtype=jnp.float32), 'b1': jnp.zeros((NUM_EXPERTS, D), dtype=jnp.float32), 'w2': jax.random.uniform(ks[3], (NUM_EXPERTS, D, D), minval=-scale_in, maxval=scale_in, dtype=jnp.float32), 'b2': jnp.zeros((NUM_EXPERTS, D), dtype=jnp.float32)}
    _L0_ffn_all = _L0_ffn_setup()
    _L0_ffn_in = {k: v for k, v in _L0_ffn_all.items() if k in ('gate_w', 'gate_b', 'w1', 'b1', 'w2', 'b2')}
    del _L0_ffn_all
    return {'x': x, 'cond_128': cond_128, 'fside_S_0': fside_S_0, 'L0_cond_weight': _L0_cond_in['weight'], 'L0_cond_c_weight': _L0_cond_in['c_weight'], 'L0_ffn_gate_w': _L0_ffn_in['gate_w'], 'L0_ffn_gate_b': _L0_ffn_in['gate_b'], 'L0_ffn_w1': _L0_ffn_in['w1'], 'L0_ffn_b1': _L0_ffn_in['b1'], 'L0_ffn_w2': _L0_ffn_in['w2'], 'L0_ffn_b2': _L0_ffn_in['b2']}

def reference(x, cond_128, fside_S_0, L0_cond_weight, L0_cond_c_weight, L0_ffn_gate_w, L0_ffn_gate_b, L0_ffn_w1, L0_ffn_b1, L0_ffn_w2, L0_ffn_b2):
    import jax
    import jax.numpy as jnp

    def _L0_cond_ref(x, c, weight, c_weight, bias):
        import jax, jax.numpy as jnp
        import numpy as np
        from jax import lax
        N, C_IN, L = (32, 64, 1024)
        C_OUT, K, GROUPS = (64, 9, 4)
        C_DIM, PAD, STRIDE = (128, 4, 1)
        out = lax.conv_general_dilated(x, weight, window_strides=(STRIDE,), padding=[(PAD, PAD)], dimension_numbers=('NCH', 'OIH', 'NCH'), feature_group_count=GROUPS)
        ctx = jnp.einsum('nd,od->no', c, c_weight)
        out = out + ctx[:, :, None] + bias[None, :, None]
        return out

    def _L0_ffn_ref(h, gate_w, gate_b, w1, b1, w2, b2):
        import jax, jax.numpy as jnp
        import numpy as np
        B, S, D = (4, 512, 1024)
        NUM_EXPERTS, TOP_K = (3, 2)

        def _expert_outputs(h, w1, b1, w2, b2):
            pre = jnp.einsum('bsd,edf->ebsf', h, w1) + b1[:, None, None, :]
            act = jnp.stack([jnp.tanh(pre[0]), jax.nn.gelu(pre[1], approximate=False), jax.nn.silu(pre[2])])
            return jnp.einsum('ebsf,efd->ebsd', act, w2) + b2[:, None, None, :]
        b, s, d = h.shape
        vision_len = int(s * 0.3)
        text_strength = jnp.mean(jnp.abs(h[:, vision_len:, :]), axis=(1, 2), keepdims=True)
        vision_strength = jnp.mean(jnp.abs(h[:, :vision_len, :]), axis=(1, 2), keepdims=True)
        modality_ratio = text_strength / (vision_strength + 1e-08)
        modality_ratio = jnp.broadcast_to(modality_ratio, (b, s, 1))
        router_input = jnp.concatenate([h, modality_ratio], axis=-1)
        gate_logits = router_input @ gate_w + gate_b
        gate_scores = jax.nn.softmax(gate_logits, axis=-1)
        top_val, top_idx = jax.lax.top_k(gate_scores, TOP_K)
        top_val = top_val / (jnp.sum(top_val, axis=-1, keepdims=True) + 1e-08)
        expert_out = _expert_outputs(h, w1, b1, w2, b2)
        moe_out = jnp.zeros_like(h)
        batch_idx = jnp.arange(b)
        for i in range(TOP_K):
            j = top_idx[:, 0, i]
            out_i = expert_out[j, batch_idx]
            moe_out = moe_out + top_val[..., i:i + 1] * out_i
        return moe_out
    x = x + _L0_ffn_ref(_L0_cond_ref(x, cond_128, L0_cond_weight, L0_cond_c_weight, fside_S_0), L0_ffn_gate_w, L0_ffn_gate_b, L0_ffn_w1, L0_ffn_b1, L0_ffn_w2, L0_ffn_b2)
    return x

_drawn_inputs = setup_inputs


def setup_inputs(seed=0):
    import zlib

    import numpy as np

    out = dict(_drawn_inputs(seed))
    spreads = {'L0_ffn_gate_b': (0.0, 0.504), 'L0_ffn_b1': (0.0, 0.798), 'L0_ffn_b2': (0.0, 0.1)}
    factors = {}
    for name, (base, spread) in spreads.items():
        noise = np.random.default_rng([zlib.crc32(name.encode()), seed]).standard_normal(out[name].shape)
        drawn = base * np.exp(spread * noise) if base else spread * noise
        out[name] = jnp.asarray(drawn.astype(out[name].dtype))
    for name, factor in factors.items():
        out[name] = (out[name] * factor).astype(out[name].dtype)
    return out
```

```python
import concourse.bass as bass
from concourse import mybir
from contextlib import ExitStack

B, C, L = 64, 64, 1024
E, D = 3, 1024
CG, K = 16, 9
NC = 128
P = 128
J = L // 2
TAPS2 = 5
VIS = int(C * 0.3)
SLOTS = 8
GROUPS = (2 * B + E * (SLOTS - 1)) // SLOTS
NSLOT = GROUPS * SLOTS
ROWS = B + SLOTS
KC = D // P
TT = SLOTS * C // P
N = SLOTS * C
UNITS = 16
RING = 4
XR = 4


def past(n, k):
    return not isinstance(n, int) or n >= k


def build(nc, x, cond, bias, conv_w, ctx_w, gate_w, gate_b, w1, b1, w2, b2, out):
    f32, f32r, i32 = mybir.dt.float32, mybir.dt.float32r, mybir.dt.int32
    ALU, ACT, AX = mybir.AluOpType, mybir.ActivationFunctionType, mybir.AxisListType
    ds = bass.ds
    ctx, conv_mem = ExitStack(), ExitStack()

    def sb(name, shape, dt=f32, mem=None):
        return (mem or ctx).enter_context(nc.sbuf_tensor(name, shape, dt))

    def sem(name):
        return ctx.enter_context(nc.semaphore(name))

    with ctx:
        h_park = nc.dram_tensor("h_park", (ROWS, P, KC * C), f32, kind="Internal").ap()
        bank = [ctx.enter_context(nc.psum_tensor(f"bank{i}", [P, 512], f32)) for i in range(8)]

        ident = sb("ident", [P, P])
        w_raw = sb("w_raw", [P, RING, 1024])
        w_hi = sb("w_hi", [P, RING, 1024], f32r)
        w_lo = sb("w_lo", [P, RING, 1024], f32r)
        h_raw = sb("h_raw", [P, SLOTS, KC * C])
        h_hi = sb("h_hi", [P, SLOTS, KC * C], f32r)
        h_lo = sb("h_lo", [P, SLOTS, KC * C], f32r)
        traits = sb("traits", [P, E, 4 + 3 * KC])
        b2_all = sb("b2_all", [P, E, D])
        stat = sb("stat", [P, B, 4])
        fold = sb("fold", [P, C])
        before = sb("before", [B, B])
        ones = sb("ones", [B, P])
        slot_no = sb("slot_no", [B, NSLOT])
        spare = sb("spare", [B, NSLOT])
        rel = sb("rel", [B, NSLOT])
        group_no = sb("group_no", [P, GROUPS])
        eights = sb("eights", [P, SLOTS])
        coefs = sb("coefs", [P, GROUPS, TT])
        table = sb("table", [1, NSLOT + GROUPS], i32)
        gate_last = sb("gate_last", [B, E])
        gate_bias = sb("gate_bias", [B, E])
        zeros = sb("zeros", [P, 1024])
        route = sb("route", [P, 2400])
        now = sb("now", [P, 4 + 3 * KC])
        coef_now = sb("coef_now", [P, TT])

        def cb(name, shape, dt=f32):
            return sb(name, shape, dt, conv_mem)
        with conv_mem:
            wn = cb("wn", [P, C, 2 * TAPS2])
            wn_t = cb("wn_t", [P, 2 * TAPS2, C])
            t_hi = cb("t_hi", [P, TAPS2, P], f32r)
            t_lo = cb("t_lo", [P, TAPS2, P], f32r)
            x_raw = cb("x_raw", [P, XR, L])
            x_hi = cb("x_hi", [P, 2, J + 4], f32r)
            x_lo = cb("x_lo", [P, 2, J + 4], f32r)
            conv = cb("conv", [P, 2, J])
            ht = cb("ht", [P, 2, KC * C])
            gate = cb("gate", [P, E, J])
            junk_l = cb("junk_l", [P, 2, E, J])
            junk_a = cb("junk_a", [P, 2, J])
            gate_row = cb("gate_row", [2, E * D])
            pick = cb("pick", [2, P])
            c_nat = cb("c_nat", [B, NC])
            cw_nat = cb("cw_nat", [P, NC])
            b1_nat = cb("b1_nat", [E * KC, P])
            c_t = cb("c_t", [P, B])
            cw_t = cb("cw_t", [P, P])
            bias_col = cb("bias_col", [P, 1])
            shift = cb("shift", [P, B])
            shift_now = cb("shift_now", [P, 2])
            stat_now = cb("stat_now", [P, 2, 4])
        zz = sb("zz", [P, 2, N])
        th = sb("th", [P, 2, N])
        ge = sb("ge", [P, 2, N])
        mix = sb("mix", [P, 2, 2, N])
        act_f = sb("act_f", [P, 2, N])
        act_hi = sb("act_hi", [P, KC, N], f32r)
        act_lo = sb("act_lo", [P, KC, N], f32r)
        acc = sb("acc", [P, TT, D])

        s_c, s_cw, s_bias, s_wn, s_gate = sem("s_c"), sem("s_cw"), sem("s_bias"), sem("s_wn"), sem("s_gate")
        s_b1, s_b2, s_gl = sem("s_b1"), sem("s_b2"), sem("s_gl")
        wn_zero, ident_done, pick_done, consts = sem("wn_zero"), sem("ident_done"), sem("pick_done"), sem("consts")
        pad_zero, pool_step, spare_rows = sem("pad_zero"), sem("pool_step"), sem("spare_rows")
        setup_tr, setup_t, setup_ctx, shift_done = sem("setup_tr"), sem("setup_t"), sem("setup_ctx"), sem("shift_done")
        dve_step = sem("dve_step")
        x_in = [sem(f"x_in{i}") for i in range(XR)]
        x_copied = sem("x_copied")
        x_hi_done, x_lo_done, conv_mm, shift_ready = sem("x_hi_done"), sem("x_lo_done"), sem("conv_mm"), sem("shift_ready")
        conv_done, abs_done, logit_done, stat_saved = sem("conv_done"), sem("abs_done"), sem("logit_done"), sem("stat_saved")
        tr_mm, ht_done = sem("tr_mm"), sem("ht_done")
        h_out = [sem(f"h_out{i}") for i in range(2)]
        fold_mm, exp_in, exp_done, pick_in, pick_mm, one_in, one_mm, routed = (
            sem("fold_mm"), sem("exp_in"), sem("exp_done"), sem("pick_in"), sem("pick_mm"), sem("one_in"), sem("one_mm"), sem("routed"))
        w_in = [sem(f"w_in{i}") for i in range(RING)]
        w_hi_done, w_lo_done, unit_mm = sem("w_hi_done"), sem("w_lo_done"), sem("unit_mm")
        h_in, h_hi_done, h_lo_done = sem("h_in"), sem("h_hi_done"), sem("h_lo_done")
        funcs_done, act_done, act_hi_done, act_lo_done = sem("funcs_done"), sem("act_done"), sem("act_hi_done"), sem("act_lo_done")
        traits_now, coef_ready = sem("traits_now"), sem("coef_ready")
        mixed, wn_turned = sem("mixed"), sem("wn_turned")
        acc_in, acc_b2, acc_done, acc_out = sem("acc_in"), sem("acc_b2"), sem("acc_done"), sem("acc_out")

        block = ctx.enter_context(nc.Block())
        L1_BANK = [0, 1, 2, 3, 0, 1, 4, 5]
        H_STEPS = {9: (0, 1), 10: (2, 3), 11: (4, 5), 13: (6, 7)}

        @block.sync
        def _(sp):
            def conv_step(n, it, j):
                if j is not None:
                    if past(n, XR):
                        sp.wait_ge(x_lo_done, n - XR + 1)
                    sp.dma_start(x_raw[0:C, j, :], x[ds(n, 1)].rearrange("b c l -> (b c) l")).then_inc(x_in[j], 16)
                    sp.dma_start(x_raw[C:P, j, 0:L - 1], x[ds(n, 1), :, 1:L].rearrange("b c l -> (b c) l")).then_inc(x_in[j], 16)
                    sp.dma_start(out[ds(n, 1)].rearrange("b c l -> (b c) l"), x[ds(n, 1)].rearrange("b c l -> (b c) l")).then_inc(x_copied, 16)
                if past(n, 3):
                    par = ((j if j is not None else n % 4) + 1) % 2
                    sp.wait_ge(ht_done, n - 2)
                    sp.dma_start(h_park[ds(n - 3, 1)].rearrange("b p n -> (b p) n"), ht[:, par, :]).then_inc(h_out[par], 16)

            for j in range(4):
                conv_step(j, 0, j)
            with sp.Fori(1, B // 4) as it:
                for j in range(4):
                    conv_step(it * 4 + j, it, j)
            for n in range(B, B + 3):
                conv_step(n, None, None)

            def row(g, s):
                return sp.value_load(table[0:1, ds(g * SLOTS + s, 1)], min_val=0, max_val=ROWS - 1)

            def load_h(g):
                for s in range(SLOTS):
                    sp.dma_start(h_raw[:, s, :], h_park[ds(row(g, s), 1)].rearrange("b p n -> (b p) n")).then_inc(h_in, 16)

            def load_acc(g):
                for s in range(SLOTS):
                    sp.dma_start(acc[C * (s % 2):C * (s % 2) + C, s // 2, :],
                                 out[ds(row(g, s), 1)].rearrange("b c l -> (b c) l")).then_inc(acc_in, 16)

            def store_acc(g):
                for s in range(SLOTS):
                    sp.dma_start(out[ds(row(g, s), 1)].rearrange("b c l -> (b c) l"),
                                 acc[C * (s % 2):C * (s % 2) + C, s // 2, :]).then_inc(acc_out, 16)

            def group(g, last=False):
                e = sp.value_load(table[0:1, ds(g + NSLOT, 1)], min_val=0, max_val=E - 1)
                for u in range(UNITS):
                    unit = g * UNITS + u
                    if past(g, 1) or u >= RING:
                        sp.wait_ge(w_lo_done, unit - RING + 1)
                    if u < 8:
                        src = w1[ds(e, 1), :, u * P:(u + 1) * P].rearrange("e (p k) f -> (e p) k f", k=KC)
                        dst = w_raw[:, u % RING, :].rearrange("p (k f) -> p k f", k=KC)
                    else:
                        k, half = (u - 8) % 4, (u - 8) // 4
                        src = w2[ds(e, 1), 2 * k * P:(2 * k + 2) * P, half * 512:(half + 1) * 512].rearrange("e (t p) d -> (e p) t d", p=P)
                        dst = w_raw[:, u % RING, :].rearrange("p (t d) -> p t d", t=2)
                    sp.dma_start(dst, src).then_inc(w_in[u % RING], 16)
                    if u == 4 and not last:
                        sp.wait_ge(h_lo_done, g * SLOTS + SLOTS)
                        load_h(g + 1)
                    if u == 9 and past(g, 1):
                        sp.wait_ge(acc_done, g * 8)
                        store_acc(g - 1)
                    if u == 11:
                        if past(g, 1):
                            sp.wait_ge(acc_out, g * 8 * 16)
                        load_acc(g)

            sp.wait_ge(h_out[0], 16 * (B // 2))
            sp.wait_ge(h_out[1], 16 * (B // 2))
            sp.wait_ge(x_copied, 16 * B)
            sp.wait_ge(spare_rows, 16 * 12)
            sp.wait_ge(routed, 2)
            load_h(0)
            group(0)
            with sp.Fori(1, GROUPS - 1) as g:
                group(g)
            group(GROUPS - 1, last=True)
            sp.wait_ge(acc_done, GROUPS * 8)
            store_acc(GROUPS - 1)
            sp.wait_ge(acc_out, GROUPS * 8 * 16)

        @block.gpsimd
        def _(pool):
            step = [0]

            def link(ins):
                step[0] += 1
                ins.then_inc(pool_step, 1)
                pool.wait_ge(pool_step, step[0])

            def diagonal(t, base, mult, pattern, cmp=ALU.not_equal):
                link(pool.affine_select(out=t, in_=t, compare_op=cmp, fill=1.0, base=base, pattern=pattern,
                                        channel_multiplier=mult))

            pool.memset(wn[:, :, :], 0.0).then_inc(wn_zero, 1)
            pool.memset(x_hi[:, :, :].bitcast(f32), 0.0).then_inc(pad_zero, 1)
            pool.memset(x_lo[:, :, :].bitcast(f32), 0.0).then_inc(pad_zero, 1)
            link(pool.memset(ident[:, :], 0.0))
            diagonal(ident[:, :], 0, 1, [[-1, P]])
            link(pool.memset(pick[:, :], 0.0))
            diagonal(pick[:, :].rearrange("p (q o) -> p q o", q=2), 0, 1, [[-1, 2], [0, C]])
            pool.memset(ones[:, :], 1.0).then_inc(ident_done, 1)
            link(pool.memset(zeros[:, :], 0.0))
            for i in range(SLOTS * C // P):
                pool.dma_start(out[B + 2 * i:B + 2 * i + 2].rearrange("b c l -> (b c) l"), zeros[:, :]).then_inc(spare_rows, 16)
            for i in range(SLOTS):
                pool.dma_start(h_park[B + i], zeros[:, 0:KC * C]).then_inc(spare_rows, 16)
            link(pool.memset(fold[:, :], 0.0))
            diagonal(fold[:, :], 0, 1, [[-1, C]])
            diagonal(fold[:, :], -C, 1, [[-1, C]])
            link(pool.memset(before[:, :], 0.0))
            diagonal(before[:, :], 0, 1, [[-1, B]], ALU.is_ge)
            kw = dict(allow_small_or_imprecise_dtypes=True)
            pool.iota(slot_no[:, :], [[1, NSLOT]], base=0, channel_multiplier=0, **kw)
            pool.iota(spare[:, :], [[0, GROUPS], [1, SLOTS]], base=B, channel_multiplier=0, **kw)
            pool.iota(rel[:, :], [[0, GROUPS], [-1, SLOTS]], base=-B, channel_multiplier=1, **kw)
            pool.iota(group_no[:, :], [[1, GROUPS]], base=0, channel_multiplier=0, **kw)
            pool.iota(eights[:, :], [[SLOTS, SLOTS]], base=0, channel_multiplier=0, **kw).then_inc(consts, 1)

            def conv_step(n, j):
                if j is not None:
                    if past(n, 2):
                        pool.wait_ge(conv_done, n - 1)
                    pool.tensor_copy(shift_now[:, j % 2:j % 2 + 1], shift[:, ds(n, 1)]).then_inc(shift_ready, 1)
                if past(n, 1):
                    par = ((j or 0) + 1) % 2
                    pool.wait_ge(abs_done, n)
                    pool.wait_ge(logit_done, n)
                    pool.tensor_copy(stat[:, ds(n - 1, 1), :].rearrange("p b k -> p (b k)"), stat_now[:, par, :]).then_inc(stat_saved, 1)

            pool.wait_ge(shift_done, 1)
            for j in range(4):
                conv_step(j, j)
            with pool.Fori(1, B // 4) as it:
                for j in range(4):
                    conv_step(it * 4 + j, j)
            conv_step(B, None)

            def group(g):
                e = pool.value_load(table[0:1, ds(g + NSLOT, 1)], min_val=0, max_val=E - 1)
                if past(g, 1):
                    pool.wait_ge(funcs_done, g * KC)
                    pool.wait_ge(act_done, g * KC)
                pool.tensor_copy(now[:, :], traits[:, ds(e, 1), :].rearrange("p e k -> p (e k)")).then_inc(traits_now, 1)
                if past(g, 1):
                    pool.wait_ge(acc_done, g * 8)
                pool.tensor_copy(coef_now[:, :], coefs[:, ds(g, 1), :].rearrange("p g k -> p (g k)")).then_inc(coef_ready, 1)

            pool.wait_ge(routed, 2)
            group(0)
            with pool.Fori(1, GROUPS) as g:
                group(g)

        @block.scalar
        def _(act):
            act.wait_ge(wn_zero, 1)
            for q in range(2):
                for gr in range(C // CG):
                    r = q * C + gr * CG
                    act.dma_start(wn[r:r + CG, gr * CG:(gr + 1) * CG, q:q + K], conv_w[gr * CG:(gr + 1) * CG]).then_inc(s_wn, 16)
            act.dma_start(c_nat[:, :], cond).then_inc(s_c, 16)
            act.dma_start(gate_row[0:1, :], gate_w[0:D, :].rearrange("(a n) e -> a (n e)", a=1)).then_inc(s_gate, 16)
            act.dma_start(gate_row[1:2, 0:E * (D - 1)], gate_w[1:D, :].rearrange("(a n) e -> a (n e)", a=1)).then_inc(s_gate, 16)
            for q in range(2):
                act.dma_start(cw_nat[q * C:(q + 1) * C, :], ctx_w).then_inc(s_cw, 16)
                act.dma_start(bias_col[q * C:(q + 1) * C, :], bias.rearrange("(n a) -> n a", a=1)).then_inc(s_bias, 16)
            act.dma_start(b1_nat[:, :], b1.rearrange("e (m f) -> (e m) f", f=P)).then_inc(s_b1, 16)
            for e in range(E):
                act.dma_start(b2_all[:, e, :], b2[e:e + 1, :].to_broadcast([P, D])).then_inc(s_b2, 16)
            act.dma_start(gate_last[:, :], gate_w[D:D + 1, :].to_broadcast([B, E])).then_inc(s_gl, 16)
            act.dma_start(gate_bias[:, :], gate_b.rearrange("(a e) -> a e", a=1).to_broadcast([B, E])).then_inc(s_gl, 16)
            act.wait_ge(pad_zero, 2)

            def conv_step(n, it, j):
                if j is not None:
                    act.wait_ge(x_in[j], it * 32 + 32)
                    if past(n, 2):
                        act.wait_ge(conv_mm, n - 1)
                    act.activation(x_hi[:, j % 2, 2:2 + J], x_raw[:, j, 0:L:2], ACT.Copy).then_inc(x_hi_done, 1)
                if past(n, 1):
                    par = ((j or 0) + 1) % 2
                    act.wait_ge(conv_mm, n)
                    act.wait_ge(shift_ready, n)
                    if past(n, 3):
                        act.wait_ge(tr_mm, n - 2)
                        act.wait_ge(logit_done, n - 2)
                    act.activation(conv[:, par, :].rearrange("m (k p) -> m k p", k=4), bank[par][:, :].rearrange("m (p k) -> m k p", k=4), ACT.Identity, bias=shift_now[:, par:par + 1]).then_inc(conv_done, 1)
                    act.wait_ge(conv_done, n)
                    if past(n, 3):
                        act.wait_ge(stat_saved, n - 2)
                    act.activation(junk_a[:, par, :], conv[:, par, :], ACT.Abs, accum_out=stat_now[:, par, 3:4]).then_inc(abs_done, 1)

            for j in range(4):
                conv_step(j, 0, j)
            with act.Fori(1, B // 4) as it:
                for j in range(4):
                    conv_step(it * 4 + j, it, j)
            conv_step(B, None, None)

            act.wait_ge(exp_in, 1)
            act.activation(route[0:B, 192:384], route[0:B, 0:192], ACT.Exp).then_inc(exp_done, 1)

            def split_h(g, s):
                act.activation(h_hi[:, s, :], h_raw[:, s, :], ACT.Copy).then_inc(h_hi_done, 1)

            def split_w(unit, it4, r):
                act.wait_ge(w_in[r], it4 * 16 + 16)
                if past(unit, RING):
                    act.wait_ge(unit_mm, unit - RING + 1)
                act.activation(w_hi[:, r, :], w_raw[:, r, :], ACT.Copy).then_inc(w_hi_done, 1)

            def group(g, last=False):
                for u in range(UNITS):
                    m = u - 1
                    if 0 <= m < KC:
                        if m == 0:
                            act.wait_ge(traits_now, g + 1)
                        act.wait_ge(unit_mm, g * UNITS + u)
                        if past(g, 1) or m >= 2:
                            act.wait_ge(act_done, g * KC + m - 1)
                        ps, par = bank[L1_BANK[m]], m % 2
                        act.activation(zz[:, par, :], ps[:, :], ACT.Identity, scale=now[:, 2:3], bias=now[:, 4 + KC + m:5 + KC + m])
                        act.activation(th[:, par, :], ps[:, :], ACT.Tanh, scale=now[:, 3:4], bias=now[:, 4 + 2 * KC + m:5 + 2 * KC + m])
                        act.activation(ge[:, par, :], ps[:, :], ACT.Gelu, bias=now[:, 4 + m:5 + m]).then_inc(funcs_done, 1)
                    if not (last and u + 3 >= UNITS):
                        split_w(g * UNITS + u + 3, g * 4 + (u + 3) // 4, (u + 3) % 4)
                    if 0 <= m < KC:
                        act.wait_ge(act_done, g * KC + m + 1)
                        act.activation(act_hi[:, m, :], act_f[:, par, :], ACT.Copy).then_inc(act_hi_done, 1)
                    if not last:
                        for s in H_STEPS.get(u, ()):
                            if s == 0:
                                act.wait_ge(h_in, g * 128 + 256)
                                act.wait_ge(unit_mm, g * UNITS + KC)
                            split_h(g + 1, s)

            act.wait_ge(h_in, 128)
            for s in range(SLOTS):
                split_h(0, s)
            for u in range(3):
                split_w(u, 0, u)
            group(0)
            with act.Fori(1, GROUPS - 1) as g:
                group(g)
            group(GROUPS - 1, last=True)

        @block.vector
        def _(dve):
            step = [0]

            def link(ins):
                step[0] += 1
                ins.then_inc(dve_step, 1)
                dve.wait_ge(dve_step, step[0])

            dve.wait_ge(s_wn, 16 * 8)
            dve.tensor_copy(wn_t[:, :, :], wn[:, :, :].rearrange("m c t -> m t c")).then_inc(wn_turned, 1)
            dve.wait_ge(setup_tr, 1)
            link(dve.tensor_copy(t_hi[:, 0:4, :], bank[4][:, :].rearrange("p (d m) -> p d m", m=P)))
            link(dve.tensor_copy(t_hi[:, 4, :], bank[5][:, 0:P]))
            dve.tensor_tensor(t_lo[:, 0:4, :], bank[4][:, :].rearrange("p (d m) -> p d m", m=P), t_hi[:, 0:4, :].bitcast(f32), ALU.subtract)
            dve.tensor_tensor(t_lo[:, 4, :], bank[5][:, 0:P], t_hi[:, 4, :].bitcast(f32), ALU.subtract)
            dve.tensor_copy(c_t[:, :], bank[5][:, P:P + B])
            dve.tensor_copy(cw_t[:, :], bank[5][:, 256:384])
            for e, trait in enumerate(((1.0, 0.0, 0.0, 1.0), (0.0, 1.0, 0.0, 1.0), (0.0, 0.0, 0.5, 0.5))):
                b1_e = bank[5][:, 448 + e * KC:448 + (e + 1) * KC]
                for k in range(4):
                    dve.memset(traits[:, e, k:k + 1], trait[k])
                dve.tensor_copy(traits[:, e, 4:4 + KC], b1_e)
                dve.tensor_scalar(traits[:, e, 4 + KC:4 + 2 * KC], b1_e, trait[2], None, ALU.mult)
                dve.tensor_scalar(traits[:, e, 4 + 2 * KC:4 + 3 * KC], b1_e, trait[3], None, ALU.mult)
            for e in range(E):
                last = dve.tensor_copy(gate[:, e, :], bank[(6, 7, 3)[e]][:, :])
            last.then_inc(setup_t, 1)
            dve.wait_ge(setup_ctx, 1)
            dve.wait_ge(s_bias, 32)
            dve.tensor_scalar(shift[:, :], bank[2][:, 0:B], bias_col[:, 0:1], None, ALU.add).then_inc(shift_done, 1)
            dve.wait_ge(pad_zero, 2)

            def conv_step(n, it, j, load=True):
                if load:
                    dve.wait_ge(x_hi_done, n + 1)
                    if past(n, 2):
                        dve.wait_ge(conv_mm, n - 1)
                    dve.tensor_tensor(x_lo[:, j % 2, 2:2 + J], x_raw[:, j, 0:L:2], x_hi[:, j % 2, 2:2 + J].bitcast(f32),
                                      ALU.subtract).then_inc(x_lo_done, 1)
                if past(n, 1):
                    par = (j + 1) % 2
                    dve.wait_ge(conv_done, n)
                    if past(n, 3):
                        dve.wait_ge(stat_saved, n - 2)
                    for e in range(E):
                        last = dve.tensor_tensor_reduce(out=junk_l[:, par, e, :], in0=conv[:, par, :], in1=gate[:, e, :], scale=1.0, scalar=0.0,
                                                        op0=ALU.mult, op1=ALU.add, accum_out=stat_now[:, par, e:e + 1])
                    last.then_inc(logit_done, 1)
                    dve.wait_ge(tr_mm, n)
                    if past(n, 3):
                        dve.wait_ge(h_out[par], it * 32 + (j - 1) // 2 * 16)
                    dve.tensor_copy(ht[:, par, :], bank[2 + par][:, :]).then_inc(ht_done, 1)

            for j in range(4):
                conv_step(j, 0, j)
            with dve.Fori(1, B // 4) as it:
                for j in range(4):
                    conv_step(it * 4 + j, it, j)
            conv_step(B, B // 4, 0, load=False)

            r = lambda a, n, rows=B: route[0:rows, a:a + n]
            lg, ex = r(0, 192), r(192, 192)
            lge, exe = [r(64 * e, C) for e in range(E)], [r(192 + 64 * e, C) for e in range(E)]
            vis, txt, ratio = r(384, 1), r(385, 1), r(386, 1)
            add = r(388, E)
            top, low, t0, t1 = r(400, C), r(464, C), r(528, C), r(592, C)
            v0, v1, rd = r(656, C), r(720, C), r(784, C)
            g10, g20, g21 = r(850, 1), r(851, 1), r(852, 1)
            rank, sel, first, second = r(856, E), r(860, E), r(864, E), r(868, E)
            tot = r(880, E, P)
            less = r(884, SLOTS, P)
            gr = r(896, E, P)
            start = r(900, E)
            slot = r(904, E)
            wt = [route[0:B, 912 + P * e:912 + P * (e + 1)] for e in range(E)]
            hot = [route[0:B, 1296 + NSLOT * e:1296 + NSLOT * (e + 1)] for e in range(E)]
            hot_rel = r(1296 + NSLOT * E, NSLOT)
            ge0, ge1, ex_g = r(1880, GROUPS, P), r(1900, GROUPS, P), r(1920, GROUPS, P)
            g01 = r(1940, 1, P)
            cut = r(2000, NSLOT, 1)
            A = bank[4]
            dve.wait_ge(fold_mm, 1)
            dve.wait_ge(s_gl, 32)
            dve.reduce_sum(vis, A[0:B, 192:192 + VIS], AX.X)
            link(dve.reduce_sum(txt, A[0:B, 192 + VIS:256], AX.X))
            link(dve.tensor_scalar(vis, vis, 1.0 / (VIS * L), 1e-8, ALU.mult, ALU.add))
            link(dve.reciprocal(vis, vis))
            link(dve.tensor_scalar(ratio, txt, 1.0 / ((C - VIS) * L), vis, ALU.mult, ALU.mult))
            link(dve.scalar_tensor_tensor(out=add, in0=gate_last[:, :], scalar=ratio, in1=gate_bias[:, :], op0=ALU.mult, op1=ALU.add))
            for e in range(E):
                last = dve.tensor_scalar(lge[e], A[0:B, 64 * e:64 * e + 64], add[:, e:e + 1], None, ALU.add)
            link(last)
            link(dve.tensor_tensor(top, lge[0], lge[1], ALU.max))
            link(dve.tensor_tensor(top, top, lge[2], ALU.max))
            for e in range(E):
                last = dve.tensor_tensor(lge[e], lge[e], top, ALU.subtract)
            link(last)
            dve.tensor_scalar(lg, lg, -87.3, None, ALU.max).then_inc(exp_in, 1)
            dve.wait_ge(exp_in, 1)
            d0, d1, d2 = (lge[e][:, 0:1] for e in range(E))
            dve.tensor_tensor(g10, d1, d0, ALU.is_gt)
            dve.tensor_tensor(g20, d2, d0, ALU.is_gt)
            link(dve.tensor_tensor(g21, d2, d1, ALU.is_gt))
            dve.tensor_tensor(rank[:, 0:1], g10, g20, ALU.add)
            link(dve.tensor_tensor(rank[:, 1:2], g21, g10, ALU.subtract))
            link(dve.tensor_tensor(rank[:, 2:3], g20, g21, ALU.add))
            link(dve.tensor_scalar(rank[:, 1:2], rank[:, 1:2], 1.0, None, ALU.add))
            link(dve.tensor_scalar(rank[:, 2:3], rank[:, 2:3], -1.0, 2.0, ALU.mult, ALU.add))
            dve.tensor_scalar(sel, rank, 1.5, None, ALU.is_lt).then_inc(pick_in, 1)
            dve.wait_ge(pick_in, 1)
            link(dve.tensor_scalar(first, rank, 0.5, None, ALU.is_lt))
            link(dve.tensor_tensor(second, sel, first, ALU.subtract))
            dve.wait_ge(exp_done, 1)
            link(dve.tensor_tensor(t0, exe[0], exe[1], ALU.add))
            link(dve.tensor_tensor(t0, t0, exe[2], ALU.add))
            link(dve.reciprocal(t0, t0))
            for e in range(E):
                last = dve.tensor_tensor(exe[e], exe[e], t0, ALU.mult)
            link(last)
            dve.tensor_tensor(top, exe[0], exe[1], ALU.max)
            link(dve.tensor_tensor(low, exe[0], exe[1], ALU.min))
            link(dve.tensor_tensor(t1, top, exe[2], ALU.min))
            dve.tensor_tensor(v0, top, exe[2], ALU.max)
            link(dve.tensor_tensor(v1, low, t1, ALU.max))
            link(dve.scalar_tensor_tensor(out=rd, in0=v0, scalar=1e-8, in1=v1, op0=ALU.add, op1=ALU.add))
            link(dve.reciprocal(rd, rd))
            dve.tensor_tensor(v0, v0, rd, ALU.mult)
            link(dve.tensor_tensor(v1, v1, rd, ALU.mult))
            for e in range(E):
                link(dve.tensor_scalar(t0, v0, first[:, e:e + 1], None, ALU.mult))
                dve.scalar_tensor_tensor(out=wt[e][:, 0:C], in0=v1, scalar=second[:, e:e + 1], in1=t0, op0=ALU.mult, op1=ALU.add)
                link(dve.scalar_tensor_tensor(out=wt[e][:, C:P], in0=v1, scalar=second[:, e:e + 1], in1=t0, op0=ALU.mult, op1=ALU.add))
            dve.wait_ge(pick_mm, 1)
            dve.wait_ge(consts, 1)
            link(dve.tensor_copy(tot, bank[5][:, 0:E]))
            for e in range(E):
                link(dve.tensor_scalar(less, eights[:, :], tot[:, e:e + 1], None, ALU.is_lt))
                link(dve.reduce_sum(gr[:, e:e + 1], less, AX.X))
            link(dve.tensor_tensor(g01, gr[:, 0:1], gr[:, 1:2], ALU.add))
            link(dve.memset(start[:, 0:1], 0.0))
            link(dve.tensor_scalar(start[:, 1:2], gr[0:B, 0:1], float(SLOTS), None, ALU.mult))
            link(dve.tensor_scalar(start[:, 2:3], g01[0:B, :], float(SLOTS), None, ALU.mult))
            link(dve.tensor_tensor(slot, bank[5][0:B, 8:8 + E], start, ALU.add))
            for e in range(E):
                link(dve.tensor_scalar(hot[e], slot_no[:, :], slot[:, e:e + 1], sel[:, e:e + 1], ALU.is_equal, ALU.mult))
            link(dve.tensor_tensor(hot_rel, hot[0], hot[1], ALU.add))
            link(dve.tensor_tensor(hot_rel, hot_rel, hot[2], ALU.add))
            dve.tensor_tensor(hot_rel, hot_rel, rel[:, :], ALU.mult).then_inc(one_in, 1)
            dve.tensor_scalar(ge0, group_no[:, :], gr[:, 0:1], None, ALU.is_ge)
            link(dve.tensor_scalar(ge1, group_no[:, :], g01, None, ALU.is_ge))
            link(dve.tensor_tensor(ex_g, ge0, ge1, ALU.add))
            dve.tensor_copy(table[0:1, NSLOT:NSLOT + GROUPS], ex_g[0:1, :]).then_inc(routed, 1)
            dve.wait_ge(one_mm, 1)
            cw = bank[6][:, 0:NSLOT].rearrange("p (g t h) -> p g t h", t=TT, h=2)
            for h in range(2):
                dve.tensor_copy(coefs[C * h:C * h + C, :, :], cw[C * h:C * h + C, :, :, h])
            dve.tensor_tensor(table[0:1, 0:NSLOT], bank[7][0:1, 0:NSLOT], spare[0:1, :], ALU.add).then_inc(routed, 1)

            def split_h(g, s):
                dve.wait_ge(h_hi_done, g * SLOTS + s + 1)
                dve.tensor_tensor(h_lo[:, s, :], h_raw[:, s, :], h_hi[:, s, :].bitcast(f32), ALU.subtract).then_inc(h_lo_done, 1)

            def split_w(unit, r):
                dve.wait_ge(w_hi_done, unit + 1)
                dve.tensor_tensor(w_lo[:, r, :], w_raw[:, r, :], w_hi[:, r, :].bitcast(f32), ALU.subtract).then_inc(w_lo_done, 1)

            def finish(g, half):
                for t in range(TT):
                    dst = acc[:, t, half * 512:(half + 1) * 512]
                    dve.scalar_tensor_tensor(out=dst, in0=bank[4 * half + t][:, :], scalar=coef_now[:, t:t + 1], in1=dst,
                                             op0=ALU.mult, op1=ALU.add).then_inc(acc_done, 1)

            def group(g, last=False):
                e = dve.value_load(table[0:1, ds(g + NSLOT, 1)], min_val=0, max_val=E - 1)
                for u in range(UNITS):
                    m = u - 1
                    if u == 0 and past(g, 1):
                        dve.wait_ge(unit_mm, g * UNITS)
                        finish(g - 1, 1)
                    if 0 <= m < KC:
                        par = m % 2
                        if m == 0:
                            dve.wait_ge(traits_now, g + 1)
                        dve.wait_ge(funcs_done, g * KC + m + 1)
                        if past(g, 1) or m >= 2:
                            dve.wait_ge(act_hi_done, g * KC + m - 1)
                        step_a = dve.scalar_tensor_tensor(out=mix[:, par, 0, :], in0=zz[:, par, :], scalar=now[:, 0:1], in1=th[:, par, :],
                                                          op0=ALU.add, op1=ALU.mult)
                        step_a.then_inc(mixed, 1)
                        dve.wait_ge(mixed, g * 16 + 2 * m + 1)
                        dve.tensor_tensor(mix[:, par, 1, :], mix[:, par, 0, :], zz[:, par, :], ALU.add).then_inc(mixed, 1)
                        dve.wait_ge(mixed, g * 16 + 2 * m + 2)
                        dve.scalar_tensor_tensor(out=act_f[:, par, :], in0=ge[:, par, :], scalar=now[:, 1:2], in1=mix[:, par, 1, :],
                                                 op0=ALU.mult, op1=ALU.add).then_inc(act_done, 1)
                    if not (last and u + 3 >= UNITS):
                        split_w(g * UNITS + u + 3, (u + 3) % 4)
                    if 0 <= m < KC:
                        dve.wait_ge(act_hi_done, g * KC + m + 1)
                        dve.tensor_tensor(act_lo[:, m, :], act_f[:, par, :], act_hi[:, m, :].bitcast(f32), ALU.subtract).then_inc(act_lo_done, 1)
                    if 8 <= u < 12:
                        t = u - 8
                        if t == 0:
                            dve.wait_ge(acc_in, g * 128 + 128)
                            dve.wait_ge(coef_ready, g + 1)
                            dve.wait_ge(s_b2, 48)
                        dve.scalar_tensor_tensor(out=acc[:, t, :], in0=b2_all[:, ds(e, 1), :].rearrange("p e d -> p (e d)"),
                                                 scalar=coef_now[:, t:t + 1], in1=acc[:, t, :], op0=ALU.mult, op1=ALU.add).then_inc(acc_b2, 1)
                    if not last:
                        for s in H_STEPS.get(u, ()):
                            split_h(g + 1, s)
                    if u == 12:
                        dve.wait_ge(unit_mm, g * UNITS + 12)
                        dve.wait_ge(acc_b2, g * TT + TT)
                        finish(g, 0)

            for s in range(SLOTS):
                split_h(0, s)
            for u in range(3):
                split_w(u, u)
            group(0)
            with dve.Fori(1, GROUPS - 1) as g:
                group(g)
            group(GROUPS - 1, last=True)
            dve.wait_ge(unit_mm, GROUPS * UNITS)
            finish(GROUPS - 1, 1)

        @block.tensor
        def _(pe):
            pe.wait_ge(ident_done, 1)
            pe.wait_ge(wn_turned, 1)
            for d in range(TAPS2):
                src = wn_t[:, 2 * d:2 * d + 2, :].rearrange("m p c -> m (p c)")
                pe.transpose(bank[4][:, d * P:(d + 1) * P] if d < 4 else bank[5][:, 0:P], src, ident[:, :])
            pe.wait_ge(s_c, 16)
            pe.transpose(bank[5][:, P:P + B], c_nat[:, :], ident[0:B, 0:B])
            pe.wait_ge(s_cw, 32)
            pe.transpose(bank[5][:, 256:384], cw_nat[:, :], ident[:, :])
            pe.wait_ge(s_b1, 16)
            pe.transpose(bank[5][:, 448:448 + E * KC], b1_nat[:, :], ident[0:E * KC, 0:E * KC])
            pe.wait_ge(s_gate, 32)
            for e in range(E):
                last = pe.matmul(bank[(6, 7, 3)[e]][:, :], pick[:, :], gate_row[:, :].rearrange("r (p k i) -> r k p i", k=4, i=2 * E)[:, :, :, e], start=True, stop=True)
            last.then_inc(setup_tr, 1)
            pe.wait_ge(setup_t, 1)
            pe.matmul(bank[2][:, 0:B], cw_t[:, :], c_t[:, :], start=True, stop=True).then_inc(setup_ctx, 1)
            pe.wait_ge(shift_done, 1)

            def conv_step(n, j):
                if j is not None:
                    par = j % 2
                    pe.wait_ge(x_lo_done, n + 1)
                    if past(n, 2):
                        pe.wait_ge(conv_done, n - 1)
                    for d in range(TAPS2):
                        for i, (a, b) in enumerate(((t_hi, x_hi), (t_hi, x_lo), (t_lo, x_hi))):
                            last = pe.matmul(bank[par][:, :], a[:, d, :], b[:, par, d:d + J],
                                             start=(d + i == 0), stop=(d == TAPS2 - 1 and i == 2))
                    last.then_inc(conv_mm, 1)
                if past(n, 1):
                    par = ((j or 0) + 1) % 2
                    pe.wait_ge(conv_done, n)
                    if past(n, 3):
                        pe.wait_ge(ht_done, n - 2)
                    for k in range(4):
                        last = pe.transpose(bank[2 + par][:, k * P:(k + 1) * P], conv[:, par, k * P:(k + 1) * P], ident[:, :])
                    last.then_inc(tr_mm, 1)

            for j in range(4):
                conv_step(j, j)
            with pe.Fori(1, B // 4) as it:
                for j in range(4):
                    conv_step(it * 4 + j, j)
            conv_step(B, None)

            pe.wait_ge(stat_saved, B)
            pe.wait_ge(consts, 1)
            for e in range(4):
                last = pe.matmul(bank[4][0:B, 64 * e:64 * e + 64], stat[:, :, e], fold[:, :], start=True, stop=True)
            last.then_inc(fold_mm, 1)
            sel = route[0:B, 860:860 + E]
            pe.wait_ge(pick_in, 1)
            pe.matmul(bank[5][:, 0:E], ones[:, :], sel, start=True, stop=True)
            pe.matmul(bank[5][0:B, 8:8 + E], before[:, :], sel, start=True, stop=True).then_inc(pick_mm, 1)
            pe.wait_ge(one_in, 1)
            for e in range(E):
                pe.matmul(bank[6][:, 0:NSLOT], route[0:B, 912 + P * e:912 + P * (e + 1)],
                          route[0:B, 1296 + NSLOT * e:1296 + NSLOT * (e + 1)], start=(e == 0), stop=(e == E - 1))
            pe.matmul(bank[7][:, 0:NSLOT], ones[:, :], route[0:B, 1296 + NSLOT * E:1296 + NSLOT * (E + 1)],
                      start=True, stop=True).then_inc(one_mm, 1)

            def group(g):
                for u in range(UNITS):
                    pe.wait_ge(w_lo_done, g * UNITS + u + 1)
                    if u < KC:
                        if u == 0:
                            pe.wait_ge(h_lo_done, g * SLOTS + SLOTS)
                            if past(g, 1):
                                pe.wait_ge(acc_done, g * 8 - 4)
                        if u == 6 and past(g, 1):
                            pe.wait_ge(acc_done, g * 8)
                        if u in (4, 5):
                            pe.wait_ge(funcs_done, g * KC + u - 3)
                        w = u % RING
                        for k in range(KC):
                            for i, (a, b) in enumerate(((w_hi, h_hi), (w_hi, h_lo), (w_lo, h_hi))):
                                last = pe.matmul(bank[L1_BANK[u]][:, :], a[:, w, k * P:(k + 1) * P], b[:, :, k * C:(k + 1) * C],
                                                 start=(k + i == 0), stop=(k == KC - 1 and i == 2))
                    else:
                        half, pair, w = (u - 8) // 4, (u - 8) % 4, u % RING
                        if u == 8:
                            pe.wait_ge(funcs_done, g * KC + 6)
                        if u == 12:
                            pe.wait_ge(funcs_done, g * KC + 8)
                        if half == 0:
                            pe.wait_ge(act_lo_done, g * KC + 2 * pair + 2)
                        for f in range(2):
                            k = 2 * pair + f
                            for t in range(TT):
                                for i, (a, b) in enumerate(((act_hi, w_hi), (act_hi, w_lo), (act_lo, w_hi))):
                                    last = pe.matmul(bank[4 * half + t][:, :], a[:, k, t * P:(t + 1) * P], b[:, w, f * 512:(f + 1) * 512],
                                                     start=(k + i == 0), stop=(k == KC - 1 and i == 2))
                    last.then_inc(unit_mm, 1)

            group(0)
            with pe.Fori(1, GROUPS) as g:
                group(g)


_INS = ["x", "cond_128", "fside_S_0", "L0_cond_weight", "L0_cond_c_weight", "L0_ffn_gate_w", "L0_ffn_gate_b",
        "L0_ffn_w1", "L0_ffn_b1", "L0_ffn_w2", "L0_ffn_b2"]


def kernel(**inputs):
    import numpy as _np
    import concourse.bacc as _bacc
    from concourse import mybir as _mybir
    from concourse.bass_utils import run_bass_kernel_spmd as _run

    nc = _bacc.Bacc("TRN2", target_bir_lowering=False, num_devices=1)
    arrays, args = {}, []
    for name in _INS:
        a = _np.ascontiguousarray(inputs[name])
        arrays[f"in_{name}_dram"] = a
        args.append(nc.dram_tensor(f"in_{name}_dram", a.shape, _mybir.dt.from_np(a.dtype), kind="ExternalInput").ap())
    args.append(nc.dram_tensor("out_0_dram", (ROWS, C, L), _mybir.dt.float32, kind="ExternalOutput").ap())
    build(nc, *args)
    r = _run(nc, [arrays], core_ids=[0])
    return r.results[0]["out_0_dram"][:B]
```

```python
import concourse.bass as bass
from concourse import mybir
from contextlib import ExitStack

B, C, L = 64, 64, 1024
E, D = 3, 1024
CG, K = 16, 9
NC = 128
P = 128
J = L // 2
TAPS2 = 5
VIS = int(C * 0.3)
SLOTS = 6
GROUPS = (2 * B + E * (SLOTS - 1)) // SLOTS
NSLOT = GROUPS * SLOTS
MOST = -(-B // SLOTS)
ROWS = B + SLOTS
KC = D // P
TT = SLOTS * C // P
N = SLOTS * C
UNITS = 16
RING = 4
XR = 4


def past(n, k):
    return not isinstance(n, int) or n >= k


def build(nc, x, cond, bias, conv_w, ctx_w, gate_w, gate_b, w1, b1, w2, b2, out):
    f32, f32r, i32 = mybir.dt.float32, mybir.dt.float32r, mybir.dt.int32
    ALU, ACT, AX = mybir.AluOpType, mybir.ActivationFunctionType, mybir.AxisListType
    ds = bass.ds
    ctx, conv_mem = ExitStack(), ExitStack()

    def sb(name, shape, dt=f32, mem=None):
        return (mem or ctx).enter_context(nc.sbuf_tensor(name, shape, dt))

    def sem(name):
        return ctx.enter_context(nc.semaphore(name))

    with ctx:
        h_park = nc.dram_tensor("h_park", (ROWS, P, KC * C), f32, kind="Internal").ap()
        bank = [ctx.enter_context(nc.psum_tensor(f"bank{i}", [P, 512], f32)) for i in range(8)]

        ident = sb("ident", [P, P])
        w_raw = sb("w_raw", [P, RING, 1024])
        w_hi = sb("w_hi", [P, RING, 1024], f32r)
        w_lo = sb("w_lo", [P, RING, 1024], f32r)
        h_raw = sb("h_raw", [P, SLOTS, KC * C])
        h_hi = sb("h_hi", [P, SLOTS, KC * C], f32r)
        h_lo = sb("h_lo", [P, SLOTS, KC * C], f32r)
        traits = sb("traits", [P, E, 4 + 3 * KC])
        b2_all = sb("b2_all", [P, E, D])
        stat = sb("stat", [P, B, 4])
        fold = sb("fold", [P, C])
        before = sb("before", [B, B])
        ones = sb("ones", [B, P])
        slot_no = sb("slot_no", [B, NSLOT])
        spare = sb("spare", [B, NSLOT])
        rel = sb("rel", [B, NSLOT])
        group_no = sb("group_no", [P, GROUPS])
        steps = sb("steps", [P, MOST])
        coefs = sb("coefs", [P, GROUPS, TT])
        table = sb("table", [1, NSLOT + GROUPS], i32)
        gate_last = sb("gate_last", [B, E])
        gate_bias = sb("gate_bias", [B, E])
        zeros = sb("zeros", [P, 1024])
        route = sb("route", [P, 2400])
        now = sb("now", [P, 4 + 3 * KC])
        coef_now = sb("coef_now", [P, TT])

        def cb(name, shape, dt=f32):
            return sb(name, shape, dt, conv_mem)
        with conv_mem:
            wn = cb("wn", [P, C, 2 * TAPS2])
            wn_t = cb("wn_t", [P, 2 * TAPS2, C])
            t_hi = cb("t_hi", [P, TAPS2, P], f32r)
            t_lo = cb("t_lo", [P, TAPS2, P], f32r)
            x_raw = cb("x_raw", [P, XR, L])
            x_hi = cb("x_hi", [P, 2, J + 4], f32r)
            x_lo = cb("x_lo", [P, 2, J + 4], f32r)
            conv = cb("conv", [P, 2, J])
            ht = cb("ht", [P, 2, KC * C])
            gate = cb("gate", [P, E, J])
            junk_l = cb("junk_l", [P, 2, E, J])
            junk_a = cb("junk_a", [P, 2, J])
            gate_row = cb("gate_row", [2, E * D])
            pick = cb("pick", [2, P])
            c_nat = cb("c_nat", [B, NC])
            cw_nat = cb("cw_nat", [P, NC])
            b1_nat = cb("b1_nat", [E * KC, P])
            c_t = cb("c_t", [P, B])
            cw_t = cb("cw_t", [P, P])
            bias_col = cb("bias_col", [P, 1])
            shift = cb("shift", [P, B])
            shift_now = cb("shift_now", [P, 2])
            stat_now = cb("stat_now", [P, 2, 4])
        zz = sb("zz", [P, 2, N])
        th = sb("th", [P, 2, N])
        ge = sb("ge", [P, 2, N])
        mix = sb("mix", [P, 2, 2, N])
        act_f = sb("act_f", [P, 2, N])
        act_hi = sb("act_hi", [P, KC, N], f32r)
        act_lo = sb("act_lo", [P, KC, N], f32r)
        acc = sb("acc", [P, TT, D])

        s_c, s_cw, s_bias, s_wn, s_gate = sem("s_c"), sem("s_cw"), sem("s_bias"), sem("s_wn"), sem("s_gate")
        s_b1, s_b2, s_gl = sem("s_b1"), sem("s_b2"), sem("s_gl")
        wn_zero, ident_done, pick_done, consts = sem("wn_zero"), sem("ident_done"), sem("pick_done"), sem("consts")
        pad_zero, pool_step, spare_rows = sem("pad_zero"), sem("pool_step"), sem("spare_rows")
        setup_tr, setup_t, setup_ctx, shift_done = sem("setup_tr"), sem("setup_t"), sem("setup_ctx"), sem("shift_done")
        dve_step = sem("dve_step")
        x_in = [sem(f"x_in{i}") for i in range(XR)]
        x_copied = sem("x_copied")
        x_hi_done, x_lo_done, conv_mm, shift_ready = sem("x_hi_done"), sem("x_lo_done"), sem("conv_mm"), sem("shift_ready")
        conv_done, abs_done, logit_done, stat_saved = sem("conv_done"), sem("abs_done"), sem("logit_done"), sem("stat_saved")
        tr_mm, ht_done = sem("tr_mm"), sem("ht_done")
        h_out = [sem(f"h_out{i}") for i in range(2)]
        fold_mm, exp_in, exp_done, pick_in, pick_mm, one_in, one_mm, routed = (
            sem("fold_mm"), sem("exp_in"), sem("exp_done"), sem("pick_in"), sem("pick_mm"), sem("one_in"), sem("one_mm"), sem("routed"))
        w_in = [sem(f"w_in{i}") for i in range(RING)]
        w_hi_done, w_lo_done, unit_mm = sem("w_hi_done"), sem("w_lo_done"), sem("unit_mm")
        h_in, h_hi_done, h_lo_done = sem("h_in"), sem("h_hi_done"), sem("h_lo_done")
        funcs_done, act_done, act_hi_done, act_lo_done = sem("funcs_done"), sem("act_done"), sem("act_hi_done"), sem("act_lo_done")
        traits_now, coef_ready = sem("traits_now"), sem("coef_ready")
        mixed, wn_turned = sem("mixed"), sem("wn_turned")
        acc_in, acc_b2, acc_done, acc_out = sem("acc_in"), sem("acc_b2"), sem("acc_done"), sem("acc_out")

        block = ctx.enter_context(nc.Block())
        L1_BANK = 2 * TT
        H_STEPS = {9: (0, 1), 10: (2, 3), 11: (4, 5)}

        @block.sync
        def _(sp):
            def conv_step(n, it, j):
                if j is not None:
                    if past(n, XR):
                        sp.wait_ge(x_lo_done, n - XR + 1)
                    sp.dma_start(x_raw[0:C, j, :], x[ds(n, 1)].rearrange("b c l -> (b c) l")).then_inc(x_in[j], 16)
                    sp.dma_start(x_raw[C:P, j, 0:L - 1], x[ds(n, 1), :, 1:L].rearrange("b c l -> (b c) l")).then_inc(x_in[j], 16)
                    if j == 0:
                        sp.dma_start(out[ds(n, XR)].rearrange("b c l -> (b c) l"), x[ds(n, XR)].rearrange("b c l -> (b c) l")).then_inc(x_copied, 16)
                if past(n, 4):
                    par = (n if j is None else j) % 2
                    sp.wait_ge(ht_done, n - 3)
                    sp.dma_start(h_park[ds(n - 4, 1)].rearrange("b p n -> (b p) n"), ht[:, par, :]).then_inc(h_out[par], 16)

            for j in range(XR):
                conv_step(j, 0, j)
            with sp.Fori(1, B // XR) as it:
                for j in range(XR):
                    conv_step(it * XR + j, it, j)
            for n in range(B, B + 4):
                conv_step(n, None, None)

            def row(g, s):
                return sp.value_load(table[0:1, ds(g * SLOTS + s, 1)], min_val=0, max_val=ROWS - 1)

            def load_h(g):
                for s in range(SLOTS):
                    sp.dma_start(h_raw[:, s, :], h_park[ds(row(g, s), 1)].rearrange("b p n -> (b p) n")).then_inc(h_in, 16)

            def load_acc(g):
                for s in range(SLOTS):
                    sp.dma_start(acc[C * (s % 2):C * (s % 2) + C, s // 2, :],
                                 out[ds(row(g, s), 1)].rearrange("b c l -> (b c) l")).then_inc(acc_in, 16)

            def store_acc(g):
                for s in range(SLOTS):
                    sp.dma_start(out[ds(row(g, s), 1)].rearrange("b c l -> (b c) l"),
                                 acc[C * (s % 2):C * (s % 2) + C, s // 2, :]).then_inc(acc_out, 16)

            def group(g, last=False):
                e = sp.value_load(table[0:1, ds(g + NSLOT, 1)], min_val=0, max_val=E - 1)
                for u in range(UNITS):
                    unit = g * UNITS + u
                    if past(g, 1) or u >= RING:
                        sp.wait_ge(w_lo_done, unit - RING + 1)
                    if u < 8:
                        src = w1[ds(e, 1), :, u * P:(u + 1) * P].rearrange("e (p k) f -> (e p) k f", k=KC)
                        dst = w_raw[:, u % RING, :].rearrange("p (k f) -> p k f", k=KC)
                    else:
                        k, half = (u - 8) % 4, (u - 8) // 4
                        src = w2[ds(e, 1), 2 * k * P:(2 * k + 2) * P, half * 512:(half + 1) * 512].rearrange("e (t p) d -> (e p) t d", p=P)
                        dst = w_raw[:, u % RING, :].rearrange("p (t d) -> p t d", t=2)
                    sp.dma_start(dst, src).then_inc(w_in[u % RING], 16)
                    if u == 4 and not last:
                        sp.wait_ge(h_lo_done, g * SLOTS + SLOTS)
                        load_h(g + 1)
                    if u == 9 and past(g, 1):
                        sp.wait_ge(acc_done, g * 2 * TT)
                        store_acc(g - 1)
                    if u == 11:
                        if past(g, 1):
                            sp.wait_ge(acc_out, g * SLOTS * 16)
                        load_acc(g)

            sp.wait_ge(h_out[0], 16 * (B // 2))
            sp.wait_ge(h_out[1], 16 * (B // 2))
            sp.wait_ge(x_copied, 16 * (B // XR))
            sp.wait_ge(spare_rows, 16 * (SLOTS * C // P + SLOTS))
            sp.wait_ge(routed, 2)
            load_h(0)
            group(0)
            with sp.Fori(1, GROUPS - 1) as g:
                group(g)
            group(GROUPS - 1, last=True)
            sp.wait_ge(acc_done, GROUPS * 2 * TT)
            store_acc(GROUPS - 1)
            sp.wait_ge(acc_out, GROUPS * SLOTS * 16)

        @block.gpsimd
        def _(pool):
            step = [0]

            def link(ins):
                step[0] += 1
                ins.then_inc(pool_step, 1)
                pool.wait_ge(pool_step, step[0])

            def diagonal(t, base, mult, pattern, cmp=ALU.not_equal):
                link(pool.affine_select(out=t, in_=t, compare_op=cmp, fill=1.0, base=base, pattern=pattern,
                                        channel_multiplier=mult))

            pool.memset(wn[:, :, :], 0.0).then_inc(wn_zero, 1)
            pool.memset(x_hi[:, :, :].bitcast(f32), 0.0).then_inc(pad_zero, 1)
            pool.memset(x_lo[:, :, :].bitcast(f32), 0.0).then_inc(pad_zero, 1)
            link(pool.memset(ident[:, :], 0.0))
            diagonal(ident[:, :], 0, 1, [[-1, P]])
            link(pool.memset(pick[:, :], 0.0))
            diagonal(pick[:, :].rearrange("p (q o) -> p q o", q=2), 0, 1, [[-1, 2], [0, C]])
            pool.memset(ones[:, :], 1.0).then_inc(ident_done, 1)
            link(pool.memset(zeros[:, :], 0.0))
            for i in range(SLOTS * C // P):
                pool.dma_start(out[B + 2 * i:B + 2 * i + 2].rearrange("b c l -> (b c) l"), zeros[:, :]).then_inc(spare_rows, 16)
            for i in range(SLOTS):
                pool.dma_start(h_park[B + i], zeros[:, 0:KC * C]).then_inc(spare_rows, 16)
            link(pool.memset(fold[:, :], 0.0))
            diagonal(fold[:, :], 0, 1, [[-1, C]])
            diagonal(fold[:, :], -C, 1, [[-1, C]])
            link(pool.memset(before[:, :], 0.0))
            diagonal(before[:, :], 0, 1, [[-1, B]], ALU.is_ge)
            kw = dict(allow_small_or_imprecise_dtypes=True)
            pool.iota(slot_no[:, :], [[1, NSLOT]], base=0, channel_multiplier=0, **kw)
            pool.iota(spare[:, :], [[0, GROUPS], [1, SLOTS]], base=B, channel_multiplier=0, **kw)
            pool.iota(rel[:, :], [[0, GROUPS], [-1, SLOTS]], base=-B, channel_multiplier=1, **kw)
            pool.iota(group_no[:, :], [[1, GROUPS]], base=0, channel_multiplier=0, **kw)
            pool.iota(steps[:, :], [[SLOTS, MOST]], base=0, channel_multiplier=0, **kw).then_inc(consts, 1)

            def conv_step(n, j):
                if j is not None:
                    if past(n, 2):
                        pool.wait_ge(conv_done, n - 1)
                    pool.tensor_copy(shift_now[:, j % 2:j % 2 + 1], shift[:, ds(n, 1)]).then_inc(shift_ready, 1)
                if past(n, 1):
                    par = ((j or 0) + 1) % 2
                    pool.wait_ge(abs_done, n)
                    pool.wait_ge(logit_done, n)
                    pool.tensor_copy(stat[:, ds(n - 1, 1), :].rearrange("p b k -> p (b k)"), stat_now[:, par, :]).then_inc(stat_saved, 1)

            pool.wait_ge(shift_done, 1)
            for j in range(4):
                conv_step(j, j)
            with pool.Fori(1, B // 4) as it:
                for j in range(4):
                    conv_step(it * 4 + j, j)
            conv_step(B, None)

            def group(g):
                e = pool.value_load(table[0:1, ds(g + NSLOT, 1)], min_val=0, max_val=E - 1)
                if past(g, 1):
                    pool.wait_ge(funcs_done, g * KC)
                    pool.wait_ge(act_done, g * KC)
                pool.tensor_copy(now[:, :], traits[:, ds(e, 1), :].rearrange("p e k -> p (e k)")).then_inc(traits_now, 1)
                if past(g, 1):
                    pool.wait_ge(acc_done, g * 2 * TT)
                pool.tensor_copy(coef_now[:, :], coefs[:, ds(g, 1), :].rearrange("p g k -> p (g k)")).then_inc(coef_ready, 1)

            pool.wait_ge(routed, 2)
            group(0)
            with pool.Fori(1, GROUPS) as g:
                group(g)

        @block.scalar
        def _(act):
            act.wait_ge(wn_zero, 1)
            for q in range(2):
                for gr in range(C // CG):
                    r = q * C + gr * CG
                    act.dma_start(wn[r:r + CG, gr * CG:(gr + 1) * CG, q:q + K], conv_w[gr * CG:(gr + 1) * CG]).then_inc(s_wn, 16)
            act.dma_start(c_nat[:, :], cond).then_inc(s_c, 16)
            act.dma_start(gate_row[0:1, :], gate_w[0:D, :].rearrange("(a n) e -> a (n e)", a=1)).then_inc(s_gate, 16)
            act.dma_start(gate_row[1:2, 0:E * (D - 1)], gate_w[1:D, :].rearrange("(a n) e -> a (n e)", a=1)).then_inc(s_gate, 16)
            for q in range(2):
                act.dma_start(cw_nat[q * C:(q + 1) * C, :], ctx_w).then_inc(s_cw, 16)
                act.dma_start(bias_col[q * C:(q + 1) * C, :], bias.rearrange("(n a) -> n a", a=1)).then_inc(s_bias, 16)
            act.dma_start(b1_nat[:, :], b1.rearrange("e (m f) -> (e m) f", f=P)).then_inc(s_b1, 16)
            for e in range(E):
                act.dma_start(b2_all[:, e, :], b2[e:e + 1, :].to_broadcast([P, D])).then_inc(s_b2, 16)
            act.dma_start(gate_last[:, :], gate_w[D:D + 1, :].to_broadcast([B, E])).then_inc(s_gl, 16)
            act.dma_start(gate_bias[:, :], gate_b.rearrange("(a e) -> a e", a=1).to_broadcast([B, E])).then_inc(s_gl, 16)
            act.wait_ge(pad_zero, 2)

            def split_x(n, it, j):
                act.wait_ge(x_in[j], it * 32 + 32)
                if past(n, 2):
                    act.wait_ge(conv_mm, n - 1)
                act.activation(x_hi[:, j % 2, 2:2 + J], x_raw[:, j, 0:L:2], ACT.Copy).then_inc(x_hi_done, 1)

            def conv_step(n, it, j):
                par = (j + 1) % 2
                if past(n, 1):
                    act.wait_ge(conv_mm, n)
                    act.wait_ge(shift_ready, n)
                    if past(n, 3):
                        act.wait_ge(tr_mm, n - 2)
                        act.wait_ge(logit_done, n - 2)
                    act.activation(conv[:, par, :].rearrange("m (k p) -> m k p", k=4), bank[par][:, :].rearrange("m (p k) -> m k p", k=4),
                                   ACT.Identity, bias=shift_now[:, par:par + 1]).then_inc(conv_done, 1)
                if not (isinstance(n, int) and n + 1 >= B):
                    split_x(n + 1, it + (j + 1) // XR, (j + 1) % XR)
                if past(n, 1):
                    act.wait_ge(conv_done, n)
                    if past(n, 3):
                        act.wait_ge(stat_saved, n - 2)
                    act.activation(junk_a[:, par, :], conv[:, par, :], ACT.Abs, accum_out=stat_now[:, par, 3:4]).then_inc(abs_done, 1)

            split_x(0, 0, 0)
            for j in range(XR):
                conv_step(j, 0, j)
            with act.Fori(1, B // XR - 1) as it:
                for j in range(XR):
                    conv_step(it * XR + j, it, j)
            for n in range(B - XR, B + 1):
                conv_step(n, n // XR, n % XR)

            act.wait_ge(exp_in, 1)
            act.activation(route[0:B, 192:384], route[0:B, 0:192], ACT.Exp).then_inc(exp_done, 1)

            def split_h(g, s):
                act.activation(h_hi[:, s, :], h_raw[:, s, :], ACT.Copy).then_inc(h_hi_done, 1)

            def split_w(unit, it4, r):
                act.wait_ge(w_in[r], it4 * 16 + 16)
                if past(unit, RING):
                    act.wait_ge(unit_mm, unit - RING + 1)
                act.activation(w_hi[:, r, :], w_raw[:, r, :], ACT.Copy).then_inc(w_hi_done, 1)

            def group(g, last=False):
                for u in range(UNITS):
                    m = u - 1
                    if 0 <= m < KC:
                        if m == 0:
                            act.wait_ge(traits_now, g + 1)
                        act.wait_ge(unit_mm, g * UNITS + u)
                        if past(g, 1) or m >= 2:
                            act.wait_ge(act_done, g * KC + m - 1)
                        ps, par = bank[L1_BANK + m % 2][:, 0:N], m % 2
                        act.activation(zz[:, par, :], ps, ACT.Identity, scale=now[:, 2:3], bias=now[:, 4 + KC + m:5 + KC + m])
                        act.activation(th[:, par, :], ps, ACT.Tanh, scale=now[:, 3:4], bias=now[:, 4 + 2 * KC + m:5 + 2 * KC + m])
                        act.activation(ge[:, par, :], ps, ACT.Gelu, bias=now[:, 4 + m:5 + m]).then_inc(funcs_done, 1)
                    if not (last and u + 3 >= UNITS):
                        split_w(g * UNITS + u + 3, g * 4 + (u + 3) // 4, (u + 3) % 4)
                    if 0 <= m < KC:
                        act.wait_ge(act_done, g * KC + m + 1)
                        act.activation(act_hi[:, m, :], act_f[:, par, :], ACT.Copy).then_inc(act_hi_done, 1)
                    if not last:
                        for s in H_STEPS.get(u, ()):
                            if s == 0:
                                act.wait_ge(h_in, (g + 2) * SLOTS * 16)
                                act.wait_ge(unit_mm, g * UNITS + KC)
                            split_h(g + 1, s)

            act.wait_ge(h_in, SLOTS * 16)
            for s in range(SLOTS):
                split_h(0, s)
            for u in range(3):
                split_w(u, 0, u)
            group(0)
            with act.Fori(1, GROUPS - 1) as g:
                group(g)
            group(GROUPS - 1, last=True)

        @block.vector
        def _(dve):
            step = [0]

            def link(ins):
                step[0] += 1
                ins.then_inc(dve_step, 1)
                dve.wait_ge(dve_step, step[0])

            dve.wait_ge(s_wn, 16 * 8)
            dve.tensor_copy(wn_t[:, :, :], wn[:, :, :].rearrange("m c t -> m t c")).then_inc(wn_turned, 1)
            dve.wait_ge(setup_tr, 1)
            link(dve.tensor_copy(t_hi[:, 0:4, :], bank[4][:, :].rearrange("p (d m) -> p d m", m=P)))
            link(dve.tensor_copy(t_hi[:, 4, :], bank[5][:, 0:P]))
            dve.tensor_tensor(t_lo[:, 0:4, :], bank[4][:, :].rearrange("p (d m) -> p d m", m=P), t_hi[:, 0:4, :].bitcast(f32), ALU.subtract)
            dve.tensor_tensor(t_lo[:, 4, :], bank[5][:, 0:P], t_hi[:, 4, :].bitcast(f32), ALU.subtract)
            dve.tensor_copy(c_t[:, :], bank[5][:, P:P + B])
            dve.tensor_copy(cw_t[:, :], bank[5][:, 256:384])
            for e, trait in enumerate(((1.0, 0.0, 0.0, 1.0), (0.0, 1.0, 0.0, 1.0), (0.0, 0.0, 0.5, 0.5))):
                b1_e = bank[5][:, 448 + e * KC:448 + (e + 1) * KC]
                for k in range(4):
                    dve.memset(traits[:, e, k:k + 1], trait[k])
                dve.tensor_copy(traits[:, e, 4:4 + KC], b1_e)
                dve.tensor_scalar(traits[:, e, 4 + KC:4 + 2 * KC], b1_e, trait[2], None, ALU.mult)
                dve.tensor_scalar(traits[:, e, 4 + 2 * KC:4 + 3 * KC], b1_e, trait[3], None, ALU.mult)
            for e in range(E):
                last = dve.tensor_copy(gate[:, e, :], bank[(6, 7, 3)[e]][:, :])
            last.then_inc(setup_t, 1)
            dve.wait_ge(setup_ctx, 1)
            dve.wait_ge(s_bias, 32)
            dve.tensor_scalar(shift[:, :], bank[2][:, 0:B], bias_col[:, 0:1], None, ALU.add).then_inc(shift_done, 1)
            dve.wait_ge(pad_zero, 2)

            def split_x(n, j):
                dve.wait_ge(x_hi_done, n + 1)
                dve.tensor_tensor(x_lo[:, j % 2, 2:2 + J], x_raw[:, j, 0:L:2], x_hi[:, j % 2, 2:2 + J].bitcast(f32),
                                  ALU.subtract).then_inc(x_lo_done, 1)

            def conv_step(n, it, j):
                par = (j + 1) % 2
                if past(n, 2):
                    dve.wait_ge(tr_mm, n - 1)
                    if past(n, 4):
                        dve.wait_ge(h_out[j % 2], it * 32 + (j - 2) // 2 * 16)
                    dve.tensor_copy(ht[:, j % 2, :], bank[2 + j % 2][:, :]).then_inc(ht_done, 1)
                if not (isinstance(n, int) and n + 1 >= B):
                    split_x(n + 1, (j + 1) % XR)
                if past(n, 1) and not (isinstance(n, int) and n > B):
                    dve.wait_ge(conv_done, n)
                    if past(n, 3):
                        dve.wait_ge(stat_saved, n - 2)
                    for e in range(E):
                        last = dve.tensor_tensor_reduce(out=junk_l[:, par, e, :], in0=conv[:, par, :], in1=gate[:, e, :], scale=1.0, scalar=0.0,
                                                        op0=ALU.mult, op1=ALU.add, accum_out=stat_now[:, par, e:e + 1])
                    last.then_inc(logit_done, 1)

            split_x(0, 0)
            for j in range(XR):
                conv_step(j, 0, j)
            with dve.Fori(1, B // XR - 1) as it:
                for j in range(XR):
                    conv_step(it * XR + j, it, j)
            for n in range(B - XR, B + 2):
                conv_step(n, n // XR, n % XR)

            r = lambda a, n, rows=B: route[0:rows, a:a + n]
            lg, ex = r(0, 192), r(192, 192)
            lge, exe = [r(64 * e, C) for e in range(E)], [r(192 + 64 * e, C) for e in range(E)]
            vis, txt, ratio = r(384, 1), r(385, 1), r(386, 1)
            add = r(388, E)
            top, low, t0, t1 = r(400, C), r(464, C), r(528, C), r(592, C)
            v0, v1, rd = r(656, C), r(720, C), r(784, C)
            g10, g20, g21 = r(850, 1), r(851, 1), r(852, 1)
            rank, sel, first, second = r(856, E), r(860, E), r(864, E), r(868, E)
            tot = r(880, E, P)
            less = r(884, MOST, P)
            gr = r(896, E, P)
            start = r(900, E)
            slot = r(904, E)
            wt = [route[0:B, 912 + P * e:912 + P * (e + 1)] for e in range(E)]
            hot = [route[0:B, 1296 + NSLOT * e:1296 + NSLOT * (e + 1)] for e in range(E)]
            hot_rel = r(1296 + NSLOT * E, NSLOT)
            ge0, ge1, ex_g = r(1860, GROUPS, P), r(1890, GROUPS, P), r(1920, GROUPS, P)
            g01 = r(1950, 1, P)
            A = bank[4]
            dve.wait_ge(fold_mm, 1)
            dve.wait_ge(s_gl, 32)
            dve.reduce_sum(vis, A[0:B, 192:192 + VIS], AX.X)
            link(dve.reduce_sum(txt, A[0:B, 192 + VIS:256], AX.X))
            link(dve.tensor_scalar(vis, vis, 1.0 / (VIS * L), 1e-8, ALU.mult, ALU.add))
            link(dve.reciprocal(vis, vis))
            link(dve.tensor_scalar(ratio, txt, 1.0 / ((C - VIS) * L), vis, ALU.mult, ALU.mult))
            link(dve.scalar_tensor_tensor(out=add, in0=gate_last[:, :], scalar=ratio, in1=gate_bias[:, :], op0=ALU.mult, op1=ALU.add))
            for e in range(E):
                last = dve.tensor_scalar(lge[e], A[0:B, 64 * e:64 * e + 64], add[:, e:e + 1], None, ALU.add)
            link(last)
            link(dve.tensor_tensor(top, lge[0], lge[1], ALU.max))
            link(dve.tensor_tensor(top, top, lge[2], ALU.max))
            for e in range(E):
                last = dve.tensor_tensor(lge[e], lge[e], top, ALU.subtract)
            link(last)
            dve.tensor_scalar(lg, lg, -87.3, None, ALU.max).then_inc(exp_in, 1)
            dve.wait_ge(exp_in, 1)
            d0, d1, d2 = (lge[e][:, 0:1] for e in range(E))
            dve.tensor_tensor(g10, d1, d0, ALU.is_gt)
            dve.tensor_tensor(g20, d2, d0, ALU.is_gt)
            link(dve.tensor_tensor(g21, d2, d1, ALU.is_gt))
            dve.tensor_tensor(rank[:, 0:1], g10, g20, ALU.add)
            link(dve.tensor_tensor(rank[:, 1:2], g21, g10, ALU.subtract))
            link(dve.tensor_tensor(rank[:, 2:3], g20, g21, ALU.add))
            link(dve.tensor_scalar(rank[:, 1:2], rank[:, 1:2], 1.0, None, ALU.add))
            link(dve.tensor_scalar(rank[:, 2:3], rank[:, 2:3], -1.0, 2.0, ALU.mult, ALU.add))
            dve.tensor_scalar(sel, rank, 1.5, None, ALU.is_lt).then_inc(pick_in, 1)
            dve.wait_ge(pick_in, 1)
            link(dve.tensor_scalar(first, rank, 0.5, None, ALU.is_lt))
            link(dve.tensor_tensor(second, sel, first, ALU.subtract))
            dve.wait_ge(exp_done, 1)
            link(dve.tensor_tensor(t0, exe[0], exe[1], ALU.add))
            link(dve.tensor_tensor(t0, t0, exe[2], ALU.add))
            link(dve.reciprocal(t0, t0))
            for e in range(E):
                last = dve.tensor_tensor(exe[e], exe[e], t0, ALU.mult)
            link(last)
            dve.tensor_tensor(top, exe[0], exe[1], ALU.max)
            link(dve.tensor_tensor(low, exe[0], exe[1], ALU.min))
            link(dve.tensor_tensor(t1, top, exe[2], ALU.min))
            dve.tensor_tensor(v0, top, exe[2], ALU.max)
            link(dve.tensor_tensor(v1, low, t1, ALU.max))
            link(dve.scalar_tensor_tensor(out=rd, in0=v0, scalar=1e-8, in1=v1, op0=ALU.add, op1=ALU.add))
            link(dve.reciprocal(rd, rd))
            dve.tensor_tensor(v0, v0, rd, ALU.mult)
            link(dve.tensor_tensor(v1, v1, rd, ALU.mult))
            for e in range(E):
                link(dve.tensor_scalar(t0, v0, first[:, e:e + 1], None, ALU.mult))
                dve.scalar_tensor_tensor(out=wt[e][:, 0:C], in0=v1, scalar=second[:, e:e + 1], in1=t0, op0=ALU.mult, op1=ALU.add)
                link(dve.scalar_tensor_tensor(out=wt[e][:, C:P], in0=v1, scalar=second[:, e:e + 1], in1=t0, op0=ALU.mult, op1=ALU.add))
            dve.wait_ge(pick_mm, 1)
            dve.wait_ge(consts, 1)
            link(dve.tensor_copy(tot, bank[5][:, 0:E]))
            for e in range(E):
                link(dve.tensor_scalar(less, steps[:, :], tot[:, e:e + 1], None, ALU.is_lt))
                link(dve.reduce_sum(gr[:, e:e + 1], less, AX.X))
            link(dve.tensor_tensor(g01, gr[:, 0:1], gr[:, 1:2], ALU.add))
            link(dve.memset(start[:, 0:1], 0.0))
            link(dve.tensor_scalar(start[:, 1:2], gr[0:B, 0:1], float(SLOTS), None, ALU.mult))
            link(dve.tensor_scalar(start[:, 2:3], g01[0:B, :], float(SLOTS), None, ALU.mult))
            link(dve.tensor_tensor(slot, bank[5][0:B, 8:8 + E], start, ALU.add))
            for e in range(E):
                link(dve.tensor_scalar(hot[e], slot_no[:, :], slot[:, e:e + 1], sel[:, e:e + 1], ALU.is_equal, ALU.mult))
            link(dve.tensor_tensor(hot_rel, hot[0], hot[1], ALU.add))
            link(dve.tensor_tensor(hot_rel, hot_rel, hot[2], ALU.add))
            dve.tensor_tensor(hot_rel, hot_rel, rel[:, :], ALU.mult).then_inc(one_in, 1)
            dve.tensor_scalar(ge0, group_no[:, :], gr[:, 0:1], None, ALU.is_ge)
            link(dve.tensor_scalar(ge1, group_no[:, :], g01, None, ALU.is_ge))
            link(dve.tensor_tensor(ex_g, ge0, ge1, ALU.add))
            dve.tensor_copy(table[0:1, NSLOT:NSLOT + GROUPS], ex_g[0:1, :]).then_inc(routed, 1)
            dve.wait_ge(one_mm, 1)
            cw = bank[6][:, 0:NSLOT].rearrange("p (g t h) -> p g t h", t=TT, h=2)
            for h in range(2):
                dve.tensor_copy(coefs[C * h:C * h + C, :, :], cw[C * h:C * h + C, :, :, h])
            dve.tensor_tensor(table[0:1, 0:NSLOT], bank[7][0:1, 0:NSLOT], spare[0:1, :], ALU.add).then_inc(routed, 1)

            def split_h(g, s):
                dve.wait_ge(h_hi_done, g * SLOTS + s + 1)
                dve.tensor_tensor(h_lo[:, s, :], h_raw[:, s, :], h_hi[:, s, :].bitcast(f32), ALU.subtract).then_inc(h_lo_done, 1)

            def split_w(unit, r):
                dve.wait_ge(w_hi_done, unit + 1)
                dve.tensor_tensor(w_lo[:, r, :], w_raw[:, r, :], w_hi[:, r, :].bitcast(f32), ALU.subtract).then_inc(w_lo_done, 1)

            def finish(g, half):
                for t in range(TT):
                    dst = acc[:, t, half * 512:(half + 1) * 512]
                    dve.scalar_tensor_tensor(out=dst, in0=bank[TT * half + t][:, :], scalar=coef_now[:, t:t + 1], in1=dst,
                                             op0=ALU.mult, op1=ALU.add).then_inc(acc_done, 1)

            def group(g, last=False):
                e = dve.value_load(table[0:1, ds(g + NSLOT, 1)], min_val=0, max_val=E - 1)
                for u in range(UNITS):
                    m = u - 1
                    if u == 0 and past(g, 1):
                        dve.wait_ge(unit_mm, g * UNITS)
                        finish(g - 1, 1)
                    if 0 <= m < KC:
                        par = m % 2
                        if m == 0:
                            dve.wait_ge(traits_now, g + 1)
                        dve.wait_ge(funcs_done, g * KC + m + 1)
                        if past(g, 1) or m >= 2:
                            dve.wait_ge(act_hi_done, g * KC + m - 1)
                        step_a = dve.scalar_tensor_tensor(out=mix[:, par, 0, :], in0=zz[:, par, :], scalar=now[:, 0:1], in1=th[:, par, :],
                                                          op0=ALU.add, op1=ALU.mult)
                        step_a.then_inc(mixed, 1)
                        dve.wait_ge(mixed, g * 16 + 2 * m + 1)
                        dve.tensor_tensor(mix[:, par, 1, :], mix[:, par, 0, :], zz[:, par, :], ALU.add).then_inc(mixed, 1)
                        dve.wait_ge(mixed, g * 16 + 2 * m + 2)
                        dve.scalar_tensor_tensor(out=act_f[:, par, :], in0=ge[:, par, :], scalar=now[:, 1:2], in1=mix[:, par, 1, :],
                                                 op0=ALU.mult, op1=ALU.add).then_inc(act_done, 1)
                    if not (last and u + 3 >= UNITS):
                        split_w(g * UNITS + u + 3, (u + 3) % 4)
                    if 0 <= m < KC:
                        dve.wait_ge(act_hi_done, g * KC + m + 1)
                        dve.tensor_tensor(act_lo[:, m, :], act_f[:, par, :], act_hi[:, m, :].bitcast(f32), ALU.subtract).then_inc(act_lo_done, 1)
                    if 8 <= u < 8 + TT:
                        t = u - 8
                        if t == 0:
                            dve.wait_ge(acc_in, (g + 1) * SLOTS * 16)
                            dve.wait_ge(coef_ready, g + 1)
                            dve.wait_ge(s_b2, 48)
                        dve.scalar_tensor_tensor(out=acc[:, t, :], in0=b2_all[:, ds(e, 1), :].rearrange("p e d -> p (e d)"),
                                                 scalar=coef_now[:, t:t + 1], in1=acc[:, t, :], op0=ALU.mult, op1=ALU.add).then_inc(acc_b2, 1)
                    if not last:
                        for s in H_STEPS.get(u, ()):
                            split_h(g + 1, s)
                    if u == 12:
                        dve.wait_ge(unit_mm, g * UNITS + 12)
                        dve.wait_ge(acc_b2, g * TT + TT)
                        finish(g, 0)

            for s in range(SLOTS):
                split_h(0, s)
            for u in range(3):
                split_w(u, u)
            group(0)
            with dve.Fori(1, GROUPS - 1) as g:
                group(g)
            group(GROUPS - 1, last=True)
            dve.wait_ge(unit_mm, GROUPS * UNITS)
            finish(GROUPS - 1, 1)

        @block.tensor
        def _(pe):
            pe.wait_ge(ident_done, 1)
            pe.wait_ge(wn_turned, 1)
            for d in range(TAPS2):
                src = wn_t[:, 2 * d:2 * d + 2, :].rearrange("m p c -> m (p c)")
                pe.transpose(bank[4][:, d * P:(d + 1) * P] if d < 4 else bank[5][:, 0:P], src, ident[:, :])
            pe.wait_ge(s_c, 16)
            pe.transpose(bank[5][:, P:P + B], c_nat[:, :], ident[0:B, 0:B])
            pe.wait_ge(s_cw, 32)
            pe.transpose(bank[5][:, 256:384], cw_nat[:, :], ident[:, :])
            pe.wait_ge(s_b1, 16)
            pe.transpose(bank[5][:, 448:448 + E * KC], b1_nat[:, :], ident[0:E * KC, 0:E * KC])
            pe.wait_ge(s_gate, 32)
            for e in range(E):
                last = pe.matmul(bank[(6, 7, 3)[e]][:, :], pick[:, :], gate_row[:, :].rearrange("r (p k i) -> r k p i", k=4, i=2 * E)[:, :, :, e], start=True, stop=True)
            last.then_inc(setup_tr, 1)
            pe.wait_ge(setup_t, 1)
            pe.matmul(bank[2][:, 0:B], cw_t[:, :], c_t[:, :], start=True, stop=True).then_inc(setup_ctx, 1)
            pe.wait_ge(shift_done, 1)

            def conv_step(n, j):
                if j is not None:
                    par = j % 2
                    pe.wait_ge(x_lo_done, n + 1)
                    if past(n, 2):
                        pe.wait_ge(conv_done, n - 1)
                    for d in range(TAPS2):
                        for i, (a, b) in enumerate(((t_hi, x_hi), (t_hi, x_lo), (t_lo, x_hi))):
                            last = pe.matmul(bank[par][:, :], a[:, d, :], b[:, par, d:d + J],
                                             start=(d + i == 0), stop=(d == TAPS2 - 1 and i == 2))
                    last.then_inc(conv_mm, 1)
                if past(n, 1):
                    par = ((j or 0) + 1) % 2
                    pe.wait_ge(conv_done, n)
                    if past(n, 3):
                        pe.wait_ge(ht_done, n - 2)
                    for k in range(4):
                        last = pe.transpose(bank[2 + par][:, k * P:(k + 1) * P], conv[:, par, k * P:(k + 1) * P], ident[:, :])
                    last.then_inc(tr_mm, 1)

            for j in range(4):
                conv_step(j, j)
            with pe.Fori(1, B // 4) as it:
                for j in range(4):
                    conv_step(it * 4 + j, j)
            conv_step(B, None)

            pe.wait_ge(stat_saved, B)
            pe.wait_ge(consts, 1)
            for e in range(4):
                last = pe.matmul(bank[4][0:B, 64 * e:64 * e + 64], stat[:, :, e], fold[:, :], start=True, stop=True)
            last.then_inc(fold_mm, 1)
            sel = route[0:B, 860:860 + E]
            pe.wait_ge(pick_in, 1)
            pe.matmul(bank[5][:, 0:E], ones[:, :], sel, start=True, stop=True)
            pe.matmul(bank[5][0:B, 8:8 + E], before[:, :], sel, start=True, stop=True).then_inc(pick_mm, 1)
            pe.wait_ge(one_in, 1)
            for e in range(E):
                pe.matmul(bank[6][:, 0:NSLOT], route[0:B, 912 + P * e:912 + P * (e + 1)],
                          route[0:B, 1296 + NSLOT * e:1296 + NSLOT * (e + 1)], start=(e == 0), stop=(e == E - 1))
            pe.matmul(bank[7][:, 0:NSLOT], ones[:, :], route[0:B, 1296 + NSLOT * E:1296 + NSLOT * (E + 1)],
                      start=True, stop=True).then_inc(one_mm, 1)

            def group(g):
                for u in range(UNITS):
                    pe.wait_ge(w_lo_done, g * UNITS + u + 1)
                    if u < KC:
                        if u == 0:
                            pe.wait_ge(h_lo_done, g * SLOTS + SLOTS)
                        if past(g, 1) or u >= 2:
                            pe.wait_ge(funcs_done, g * KC + u - 1)
                        w = u % RING
                        for k in range(KC):
                            for i, (a, b) in enumerate(((w_hi, h_hi), (w_hi, h_lo), (w_lo, h_hi))):
                                last = pe.matmul(bank[L1_BANK + u % 2][:, 0:N], a[:, w, k * P:(k + 1) * P], b[:, :, k * C:(k + 1) * C],
                                                 start=(k + i == 0), stop=(k == KC - 1 and i == 2))
                    else:
                        half, pair, w = (u - 8) // 4, (u - 8) % 4, u % RING
                        if u in (8, 12) and past(g, 1):
                            pe.wait_ge(acc_done, (g * 2 + half - 1) * TT)
                        if half == 0:
                            pe.wait_ge(act_lo_done, g * KC + 2 * pair + 2)
                        for f in range(2):
                            k = 2 * pair + f
                            for t in range(TT):
                                for i, (a, b) in enumerate(((act_hi, w_hi), (act_hi, w_lo), (act_lo, w_hi))):
                                    last = pe.matmul(bank[TT * half + t][:, :], a[:, k, t * P:(t + 1) * P], b[:, w, f * 512:(f + 1) * 512],
                                                     start=(k + i == 0), stop=(k == KC - 1 and i == 2))
                    last.then_inc(unit_mm, 1)

            group(0)
            with pe.Fori(1, GROUPS) as g:
                group(g)


_INS = ["x", "cond_128", "fside_S_0", "L0_cond_weight", "L0_cond_c_weight", "L0_ffn_gate_w", "L0_ffn_gate_b",
        "L0_ffn_w1", "L0_ffn_b1", "L0_ffn_w2", "L0_ffn_b2"]


def kernel(**inputs):
    import numpy as _np
    import concourse.bacc as _bacc
    from concourse import mybir as _mybir
    from concourse.bass_utils import run_bass_kernel_spmd as _run

    nc = _bacc.Bacc("TRN2", target_bir_lowering=False, num_devices=1)
    arrays, args = {}, []
    for name in _INS:
        a = _np.ascontiguousarray(inputs[name])
        arrays[f"in_{name}_dram"] = a
        args.append(nc.dram_tensor(f"in_{name}_dram", a.shape, _mybir.dt.from_np(a.dtype), kind="ExternalInput").ap())
    args.append(nc.dram_tensor("out_0_dram", (ROWS, C, L), _mybir.dt.float32, kind="ExternalOutput").ap())
    build(nc, *args)
    r = _run(nc, [arrays], core_ids=[0])
    return r.results[0]["out_0_dram"][:B]
```

```python
import concourse.bass as bass
from concourse import mybir
from contextlib import ExitStack

B, C, L = 64, 64, 1024
E, D = 3, 1024
CG, K = 16, 9
NC = 128
P = 128
J = L // 2
TAPS2 = 5
VIS = int(C * 0.3)
SLOTS, FEW = 6, 4
SIXES, FOURS = 20, 3
GROUPS = SIXES + FOURS
NSLOT = SIXES * SLOTS + FOURS * FEW
EARLY = 24
CUTS = (FOURS + 1) ** 2
MOST = -(-B // SLOTS)
ROWS = B + SLOTS
KC = D // P
TT = SLOTS * C // P
N = SLOTS * C
UNITS = 16
RING = 4
XR = 4


def past(n, k):
    return not isinstance(n, int) or n >= k


def size(g):
    return FEW if isinstance(g, int) and g >= SIXES else SLOTS


def slots_before(g):
    return SIXES * SLOTS + (g - SIXES) * FEW if isinstance(g, int) and g >= SIXES else g * SLOTS


def tiles_before(g):
    return (SIXES * SLOTS + (g - SIXES) * FEW) // 2 if isinstance(g, int) and g >= SIXES else g * TT


def fits():
    cuts = [(i, j, FOURS - i - j) for i in range(FOURS + 1) for j in range(FOURS + 1 - i)]
    large = lambda n, f: max(0, -(-(n - FEW * f) // SLOTS))
    return all(any(large(a - SLOTS, cut[0]) + large(b, cut[1]) + large(2 * B - a - b, cut[2]) <= SIXES - 1 for cut in cuts)
               for a in range(-(-2 * EARLY // E), B + 1) for b in range(B - a, B + 1))


assert fits()


def build(nc, x, cond, bias, conv_w, ctx_w, gate_w, gate_b, w1, b1, w2, b2, out):
    f32, f32r, i32 = mybir.dt.float32, mybir.dt.float32r, mybir.dt.int32
    ALU, ACT, AX = mybir.AluOpType, mybir.ActivationFunctionType, mybir.AxisListType
    ds = bass.ds
    ctx, conv_mem = ExitStack(), ExitStack()

    def sb(name, shape, dt=f32, mem=None):
        return (mem or ctx).enter_context(nc.sbuf_tensor(name, shape, dt))

    def sem(name):
        return ctx.enter_context(nc.semaphore(name))

    with ctx:
        h_park = nc.dram_tensor("h_park", (ROWS, P, KC * C), f32, kind="Internal").ap()
        bank = [ctx.enter_context(nc.psum_tensor(f"bank{i}", [P, 512], f32)) for i in range(8)]

        ident = sb("ident", [P, P])
        w_raw = sb("w_raw", [P, RING, 1024])
        w_hi = sb("w_hi", [P, RING, 1024], f32r)
        w_lo = sb("w_lo", [P, RING, 1024], f32r)
        h_raw = sb("h_raw", [P, SLOTS, KC * C])
        h_hi = sb("h_hi", [P, SLOTS, KC * C], f32r)
        h_lo = sb("h_lo", [P, SLOTS, KC * C], f32r)
        traits = sb("traits", [P, E, 4 + 3 * KC])
        b2_all = sb("b2_all", [P, E, D])
        stat = sb("stat", [P, B, 4])
        fold = sb("fold", [P, C])
        before = sb("before", [B, B])
        ones = sb("ones", [B, P])
        slot_no = sb("slot_no", [B, NSLOT])
        spare = sb("spare", [B, NSLOT])
        rel = sb("rel", [B, NSLOT])
        group_no = sb("group_no", [P, GROUPS - 1])
        steps = sb("steps", [P, MOST])
        plan = sb("plan", [P, 2 * E, CUTS])
        rank = sb("rank", [P, CUTS])
        coefs = sb("coefs", [P, NSLOT // 2])
        table = sb("table", [1, NSLOT + GROUPS], i32)
        gate_last = sb("gate_last", [B, E])
        gate_bias = sb("gate_bias", [B, E])
        zeros = sb("zeros", [P, 1024])
        route = sb("route", [P, 3120])
        now = sb("now", [P, 4 + 3 * KC])
        early = sb("early", [B, E])
        early_slot = sb("early_slot", [B, E])
        coef_now = sb("coef_now", [P, TT])

        def cb(name, shape, dt=f32):
            return sb(name, shape, dt, conv_mem)
        with conv_mem:
            w_nat = cb("w_nat", [P, CG, K])
            of_group = cb("of_group", [P, 2 * C // CG])
            w_blocks = cb("w_blocks", [P, 2 * TAPS2, C])
            t_hi = cb("t_hi", [P, TAPS2, P], f32r)
            t_lo = cb("t_lo", [P, TAPS2, P], f32r)
            x_raw = cb("x_raw", [P, XR, L])
            x_hi = cb("x_hi", [P, 2, J + 4], f32r)
            x_lo = cb("x_lo", [P, 2, J + 4], f32r)
            conv = cb("conv", [P, 2, J])
            ht = cb("ht", [P, 2, KC * C])
            gate = cb("gate", [P, E, J])
            junk_l = cb("junk_l", [P, 2, E, J])
            junk_a = cb("junk_a", [P, 2, J])
            gate_row = cb("gate_row", [P, E * D])
            c_nat = cb("c_nat", [B, NC])
            cw_nat = cb("cw_nat", [P, NC])
            b1_nat = cb("b1_nat", [E * KC, P])
            c_t = cb("c_t", [P, B])
            cw_t = cb("cw_t", [P, P])
            bias_col = cb("bias_col", [P, 1])
            shift = cb("shift", [P, B])
            shift_now = cb("shift_now", [P, 2])
            stat_now = cb("stat_now", [P, 2, 4])
        zz = sb("zz", [P, 2, N])
        th = sb("th", [P, 2, N])
        ge = sb("ge", [P, 2, N])
        mix = sb("mix", [P, 2, 2, N])
        act_f = sb("act_f", [P, 2, N])
        act_hi = sb("act_hi", [P, KC, N], f32r)
        act_lo = sb("act_lo", [P, KC, N], f32r)
        acc = sb("acc", [P, TT, D])

        s_c, s_cw, s_bias, s_wn, s_gate = sem("s_c"), sem("s_cw"), sem("s_bias"), sem("s_wn"), sem("s_gate")
        s_b1, s_b2, s_gl = sem("s_b1"), sem("s_b2"), sem("s_gl")
        of_group_done, ident_done, consts, zeros_done = sem("of_group_done"), sem("ident_done"), sem("consts"), sem("zeros_done")
        pad_zero, pool_step, spare_rows = sem("pad_zero"), sem("pool_step"), sem("spare_rows")
        blocks_done, blocks_tr, small_tr, small_done, ctx_mm, shift_done, gate_done = (
            sem("blocks_done"), sem("blocks_tr"), sem("small_tr"), sem("small_done"), sem("ctx_mm"), sem("shift_done"), sem("gate_done"))
        dve_step, b1_tr, scores_in, last_out = sem("dve_step"), sem("b1_tr"), sem("scores_in"), sem("last_out")
        x_in = [sem(f"x_in{i}") for i in range(XR)]
        x_copied = sem("x_copied")
        x_hi_done, x_lo_done, conv_mm, shift_ready = sem("x_hi_done"), sem("x_lo_done"), sem("conv_mm"), sem("shift_ready")
        conv_done, abs_done, logit_done, stat_saved = sem("conv_done"), sem("abs_done"), sem("logit_done"), sem("stat_saved")
        tr_mm, ht_done = sem("tr_mm"), sem("ht_done")
        h_out = [sem(f"h_out{i}") for i in range(2)]
        fold_mm, exp_in, exp_done, pick_in, pick_mm, row_in, row_mm, hot_in, hot_mm, routed, early_routed = (
            sem("fold_mm"), sem("exp_in"), sem("exp_done"), sem("pick_in"), sem("pick_mm"), sem("row_in"), sem("row_mm"), sem("hot_in"), sem("hot_mm"), sem("routed"), sem("early_routed"))
        w_in = [sem(f"w_in{i}") for i in range(RING)]
        h_in = [sem(f"h_in{i}") for i in range(SLOTS)]
        w_hi_done, w_lo_done, unit_mm = sem("w_hi_done"), sem("w_lo_done"), sem("unit_mm")
        h_hi_done, h_lo_done = sem("h_hi_done"), sem("h_lo_done")
        two_done, funcs_done, act_done, act_hi_done, act_lo_done = sem("two_done"), sem("funcs_done"), sem("act_done"), sem("act_hi_done"), sem("act_lo_done")
        traits_now, coef_ready = sem("traits_now"), sem("coef_ready")
        mixed = sem("mixed")
        acc_in, acc_b2, acc_done, acc_out = sem("acc_in"), sem("acc_b2"), sem("acc_done"), sem("acc_out")

        block = ctx.enter_context(nc.Block())
        HOT, ROW, SEL, REST = 1296, 2060, 860, 872
        L1_BANK = 2 * TT
        H_STEPS = {9: (0, 2), 10: (2, 4), 11: (4, 6)}
        H_STEPS_0 = {13: (0, 2), 14: (2, 4), 15: (4, 6)}
        POOL_UNITS = range(1, 14, 2)
        H_EARLY = {B - 4: (0,), B - 3: (1,), B - 2: (2, 3), B - 1: (4, 5)}
        EARLY_AT = EARLY // 4 + 1

        @block.sync
        def _(sp):
            sp.dma_start(w_nat[0:C], conv_w).then_inc(s_wn, 16)

            def conv_step(n, it, j):
                if j is not None:
                    if past(n, XR):
                        sp.wait_ge(x_lo_done, n - XR + 1)
                    sp.dma_start(x_raw[0:C, j, :], x[ds(n, 1)].rearrange("b c l -> (b c) l")).then_inc(x_in[j], 16)
                    sp.dma_start(x_raw[C:P, j, 0:L - 1], x[ds(n, 1), :, 1:L].rearrange("b c l -> (b c) l")).then_inc(x_in[j], 16)
                    if j == XR - 1:
                        sp.dma_start(out[ds(n - j, XR)].rearrange("b c l -> (b c) l"),
                                     x[ds(n - j, XR)].rearrange("b c l -> (b c) l")).then_inc(x_copied, 16)
                if past(n, 4):
                    par = (n if j is None else j) % 2
                    sp.wait_ge(ht_done, n - 3)
                    sp.dma_start(h_park[ds(n - 4, 1)].rearrange("b p n -> (b p) n"), ht[:, par, :]).then_inc(h_out[par], 16)

            conv_step(0, 0, 0)
            conv_step(1, 0, 1)
            for q in range(2):
                sp.dma_start(bias_col[q * C:(q + 1) * C, :], bias.rearrange("(n a) -> n a", a=1)).then_inc(s_bias, 16)
            gate_flat = gate_w.rearrange("(a n) e -> a (n e)", a=1)
            for q in range(2):
                sp.dma_start(gate_row[q * C:(q + 1) * C, 0:E * (D - 1)],
                             gate_flat[:, E * q:E * (q + D - 1)].to_broadcast([C, E * (D - 1)])).then_inc(s_gate, 16)
            conv_step(2, 0, 2)
            conv_step(3, 0, 3)
            sp.dma_start(b1_nat[:, :], b1.rearrange("e (m f) -> (e m) f", f=P)).then_inc(s_b1, 16)
            sp.dma_start(gate_last[:, :], gate_w[D:D + 1, :].to_broadcast([B, E])).then_inc(s_gl, 16)
            sp.dma_start(gate_bias[:, :], gate_b.rearrange("(a e) -> a e", a=1).to_broadcast([B, E])).then_inc(s_gl, 16)
            with sp.Fori(1, B // XR - 1) as it:
                for j in range(XR):
                    conv_step(it * XR + j, it, j)

            def row(g, s):
                return sp.value_load(table[0:1, ds(slots_before(g) + s, 1)], min_val=0, max_val=ROWS - 1)

            def load_h(g, slots=None):
                for s in slots or range(size(g)):
                    sp.dma_start(h_raw[:, s, :], h_park[ds(row(g, s), 1)].rearrange("b p n -> (b p) n")).then_inc(h_in[s], 16)

            def load_w(e, u):
                if u < 8:
                    src = w1[ds(e, 1), :, u * P:(u + 1) * P].rearrange("e (p k) f -> (e p) k f", k=KC)
                    dst = w_raw[:, u % RING, :].rearrange("p (k f) -> p k f", k=KC)
                else:
                    k, half = (u - 8) % 4, (u - 8) // 4
                    src = w2[ds(e, 1), 2 * k * P:(2 * k + 2) * P, half * 512:(half + 1) * 512].rearrange("e (t p) d -> (e p) t d", p=P)
                    dst = w_raw[:, u % RING, :].rearrange("p (t d) -> p t d", t=2)
                sp.dma_start(dst, src).then_inc(w_in[u % RING], 16)

            sp.wait_ge(early_routed, 2)
            for par in range(2):
                sp.wait_ge(h_out[par], 16 * (EARLY // 2))
            e = sp.value_load(table[0:1, NSLOT:NSLOT + 1], min_val=0, max_val=E - 1)
            for j in range(XR):
                conv_step(B - XR + j, B // XR - 1, j)
                if j < SLOTS // 2:
                    load_h(0, (2 * j, 2 * j + 1))
            load_w(e, 0)
            for u in range(RING):
                if u + 1 < RING:
                    load_w(e, u + 1)
                conv_step(B + u, None, None)


            def load_acc(g):
                for s in range(size(g)):
                    sp.dma_start(acc[C * (s % 2):C * (s % 2) + C, s // 2, :],
                                 out[ds(row(g, s), 1)].rearrange("b c l -> (b c) l")).then_inc(acc_in, 16)

            def store_acc(g, slots=None, cols=slice(0, D)):
                for s in slots or range(size(g)):
                    sp.dma_start(out[ds(row(g, s), 1), :, cols].rearrange("b c l -> (b c) l"),
                                 acc[C * (s % 2):C * (s % 2) + C, s // 2, cols]).then_inc(acc_out, 16)

            def group(g, first=False, last=False):
                e = sp.value_load(table[0:1, ds(g + NSLOT, 1)], min_val=0, max_val=E - 1)
                for u in range(UNITS):
                    unit = g * UNITS + u
                    if past(g, 1) or u >= RING:
                        sp.wait_ge(w_lo_done, unit - RING + 1)
                    if not (first and u < RING):
                        load_w(e, u)
                    if first and u == RING:
                        for i in range(E):
                            sp.dma_start(b2_all[:, i, :], b2[i:i + 1, :].to_broadcast([P, D])).then_inc(s_b2, 16)
                    if first and u == 6:
                        sp.wait_ge(zeros_done, 1)
                        for i in range(SLOTS):
                            sp.dma_start(h_park[B + i], zeros[:, 0:KC * C]).then_inc(spare_rows, 16)
                    if first and u == 8:
                        for i in range(SLOTS * C // P):
                            sp.dma_start(out[B + 2 * i:B + 2 * i + 2].rearrange("b c l -> (b c) l"), zeros[:, :]).then_inc(spare_rows, 16)
                    if u == (15 if first else 6) and not last:
                        if first:
                            sp.wait_ge(h_out[0], 16 * (B // 2))
                            sp.wait_ge(h_out[1], 16 * (B // 2))
                            sp.wait_ge(spare_rows, 16 * (SLOTS * C // P + SLOTS))
                            sp.wait_ge(routed, 2)
                        sp.wait_ge(h_lo_done, slots_before(g + 1))
                        load_h(g + 1)
                    if u == 9 and past(g, 1):
                        sp.wait_ge(acc_done, 2 * tiles_before(g))
                        store_acc(g - 1)
                    if u == 11:
                        if first:
                            sp.wait_ge(x_copied, 16 * (B // XR))
                        if past(g, 1):
                            sp.wait_ge(acc_out, slots_before(g) * 16)
                        load_acc(g)

            group(0, first=True)
            with sp.Fori(1, SIXES - 1) as g:
                group(g)
            for g in range(SIXES - 1, GROUPS):
                group(g, last=g == GROUPS - 1)
            sp.wait_ge(acc_done, 2 * tiles_before(GROUPS) - FEW // 2)
            store_acc(GROUPS - 1, cols=slice(0, 512))
            sp.wait_ge(acc_done, 2 * tiles_before(GROUPS) - 1)
            store_acc(GROUPS - 1, (0, 1), slice(512, D))
            sp.wait_ge(acc_out, (NSLOT + 2) * 16)
            sp.wait_ge(last_out, (FEW - 2) * 16)

        @block.gpsimd
        def _(pool):
            step = [0]

            def link(ins):
                step[0] += 1
                ins.then_inc(pool_step, 1)
                pool.wait_ge(pool_step, step[0])

            def select(t, fill, base, mult, pattern, cmp=ALU.not_equal):
                link(pool.affine_select(out=t, in_=t, compare_op=cmp, fill=fill, base=base, pattern=pattern, channel_multiplier=mult))

            link(pool.memset(of_group[:, :], 1.0))
            grp = of_group[:, :].rearrange("p (q g) -> p q g", q=2)
            select(grp, 0.0, 0, 1, [[-C, 2], [-CG, C // CG]], ALU.is_ge)
            pool.affine_select(out=grp, in_=grp, compare_op=ALU.is_ge, fill=0.0, base=CG - 1, pattern=[[C, 2], [CG, C // CG]],
                               channel_multiplier=-1).then_inc(of_group_done, 1)
            link(pool.memset(ident[:, :], 0.0))
            pool.affine_select(out=ident[:, :], in_=ident[:, :], compare_op=ALU.not_equal, fill=1.0, base=0, pattern=[[-1, P]],
                               channel_multiplier=1).then_inc(ident_done, 1)
            for t in (x_hi, x_lo):
                pool.memset(t[:, :, 0:2].bitcast(f32), 0.0)
                pool.memset(t[:, :, J + 2:J + 4].bitcast(f32), 0.0).then_inc(pad_zero, 1)
            pool.memset(zeros[:, :], 0.0).then_inc(zeros_done, 1)

            def conv_step(n, j):
                if j is not None:
                    if past(n, 2):
                        pool.wait_ge(conv_done, n - 1)
                    pool.tensor_copy(shift_now[:, j % 2:j % 2 + 1], shift[:, ds(n, 1)]).then_inc(shift_ready, 1)
                if past(n, 1):
                    par = ((j or 0) + 1) % 2
                    pool.wait_ge(abs_done, n)
                    pool.wait_ge(logit_done, n)
                    pool.tensor_copy(stat[:, ds(n - 1, 1), :].rearrange("p b k -> p (b k)"), stat_now[:, par, :]).then_inc(stat_saved, 1)

            pool.wait_ge(shift_done, 1)
            for j in range(4):
                conv_step(j, j)
            link(pool.memset(fold[:, :], 0.0))
            select(fold[:, :], 1.0, 0, 1, [[-1, C]])
            select(fold[:, :], 1.0, -C, 1, [[-1, C]])
            link(pool.memset(before[:, :], 0.0))
            select(before[:, :], 1.0, 0, 1, [[-1, B]], ALU.is_ge)
            kw = dict(allow_small_or_imprecise_dtypes=True)
            pool.memset(ones[:, :], 1.0)
            pool.iota(slot_no[:, :], [[1, NSLOT]], base=1, channel_multiplier=0, **kw)
            for groups, slots, at in ((SIXES, SLOTS, 0), (FOURS, FEW, SIXES * SLOTS)):
                part = slice(at, at + groups * slots)
                pool.iota(spare[:, part], [[0, groups], [1, slots]], base=B, channel_multiplier=0, **kw)
                pool.iota(rel[:, part], [[0, groups], [-1, slots]], base=-B, channel_multiplier=1, **kw)
            pool.iota(group_no[:, 0:SIXES - 1], [[1, SIXES - 1]], base=0, channel_multiplier=0, **kw)
            pool.iota(group_no[:, SIXES - 1:GROUPS - 1], [[FEW, FOURS]], base=0, channel_multiplier=0, **kw)
            two = [[-1, FOURS + 1], [-1, FOURS + 1]]
            pool.iota(plan[:, E, :], [[FEW, FOURS + 1], [0, FOURS + 1]], base=0, channel_multiplier=0, **kw)
            pool.iota(plan[:, E + 1, :], [[0, FOURS + 1], [FEW, FOURS + 1]], base=0, channel_multiplier=0, **kw)
            pool.iota(plan[:, E + 2, :], [[-FEW, FOURS + 1], [-FEW, FOURS + 1]], base=FOURS * FEW, channel_multiplier=0, **kw)
            link(pool.iota(rank[:, :], [[-1, CUTS]], base=CUTS, channel_multiplier=0, **kw))
            link(pool.affine_select(out=rank[:, :].rearrange("p (i j) -> p i j", j=FOURS + 1), in_=rank[:, :].rearrange("p (i j) -> p i j", j=FOURS + 1),
                                    compare_op=ALU.is_ge, fill=0.0, base=FOURS, pattern=two, channel_multiplier=0))
            pool.iota(steps[:, :], [[SLOTS, MOST]], base=0, channel_multiplier=0, **kw).then_inc(consts, 1)
            with pool.Fori(1, B // 4) as it:
                for j in range(4):
                    conv_step(it * 4 + j, j)

            def split_w(u):
                pool.wait_ge(w_hi_done, u + 1)
                pool.wait_ge(w_lo_done, u)
                pool.tensor_tensor(w_lo[:, u % RING, :], w_raw[:, u % RING, :], w_hi[:, u % RING, :].bitcast(f32), ALU.subtract).then_inc(w_lo_done, 1)

            def split_act(m):
                pool.wait_ge(act_hi_done, m + 1)
                pool.tensor_tensor(act_lo[:, m, :], act_f[:, m % 2, :], act_hi[:, m, :].bitcast(f32), ALU.subtract).then_inc(act_lo_done, 1)

            def group(g, first=False):
                e = pool.value_load(table[0:1, ds(g + NSLOT, 1)], min_val=0, max_val=E - 1)
                if past(g, 1):
                    pool.wait_ge(funcs_done, g * KC)
                    pool.wait_ge(act_done, g * KC)
                pool.tensor_copy(now[:, :], traits[:, ds(e, 1), :].rearrange("p e k -> p (e k)")).then_inc(traits_now, 1)
                if first:
                    pool.wait_ge(h_out[0], 16 * (B // 2))
                    pool.wait_ge(h_out[1], 16 * (B // 2))
                    for u in range(11):
                        if u + 3 in POOL_UNITS:
                            split_w(u + 3)
                        if 1 <= u <= KC:
                            split_act(u - 1)
                    pool.wait_ge(routed, 3)
                if past(g, 1):
                    pool.wait_ge(acc_done, 2 * tiles_before(g))
                pool.tensor_copy(coef_now[:, 0:size(g) // 2], coefs[:, ds(tiles_before(g), size(g) // 2)]).then_inc(coef_ready, 1)
                if first:
                    for s in range(1, SLOTS, 2):
                        pool.wait_ge(h_hi_done, SLOTS + s + 1)
                        pool.tensor_tensor(h_lo[:, s, :], h_raw[:, s, :], h_hi[:, s, :].bitcast(f32), ALU.subtract).then_inc(h_lo_done, 1)

            split_w(1)
            conv_step(B, None)
            pool.wait_ge(early_routed, 2)
            group(0, first=True)
            with pool.Fori(1, SIXES) as g:
                group(g)
            for g in range(SIXES, GROUPS):
                group(g)

        @block.scalar
        def _(act):
            act.dma_start(w_nat[C:P], conv_w).then_inc(s_wn, 16)
            act.dma_start(c_nat[:, :], cond).then_inc(s_c, 16)
            for q in range(2):
                act.dma_start(cw_nat[q * C:(q + 1) * C, :], ctx_w).then_inc(s_cw, 16)

            def split_x(n, it, j):
                act.wait_ge(x_in[j], it * 32 + 32)
                if past(n, 2):
                    act.wait_ge(conv_mm, n - 1)
                act.activation(x_hi[:, j % 2, 2:2 + J], x_raw[:, j, 0:L:2], ACT.Copy).then_inc(x_hi_done, 1)

            def conv_step(n, it, j):
                par = (j + 1) % 2
                if past(n, 1):
                    act.wait_ge(conv_mm, n)
                    act.wait_ge(shift_ready, n)
                    if past(n, 3):
                        act.wait_ge(tr_mm, n - 2)
                        act.wait_ge(logit_done, n - 2)
                    act.activation(conv[:, par, :].rearrange("m (k p) -> m k p", k=4), bank[par][:, :].rearrange("m (p k) -> m k p", k=4),
                                   ACT.Identity, bias=shift_now[:, par:par + 1]).then_inc(conv_done, 1)
                if not (isinstance(n, int) and n + 1 >= B):
                    split_x(n + 1, it + (j + 1) // XR, (j + 1) % XR)
                if past(n, 1):
                    act.wait_ge(conv_done, n)
                    if past(n, 3):
                        act.wait_ge(stat_saved, n - 2)
                    act.activation(junk_a[:, par, :], conv[:, par, :], ACT.Abs, accum_out=stat_now[:, par, 3:4]).then_inc(abs_done, 1)

            split_x(0, 0, 0)
            conv_step(0, 0, 0)
            act.wait_ge(s_gate, 32)
            for e in range(E):
                for k in range(4):
                    at = 6 * k + e
                    last = act.activation(gate[:, e, k * P:(k + 1) * P], gate_row[:, at:at + 24 * (P - 1) + 1:24], ACT.Copy)
            last.then_inc(gate_done, 1)
            for j in range(1, XR):
                conv_step(j, 0, j)
            with act.Fori(1, B // XR - 1) as it:
                for j in range(XR):
                    conv_step(it * XR + j, it, j)
            def split_h(g, s):
                act.wait_ge(h_in[s], g * 16 + 16)
                act.activation(h_hi[:, s, :], h_raw[:, s, :], ACT.Copy).then_inc(h_hi_done, 1)

            def split_w(unit, it4, r):
                act.wait_ge(w_in[r], it4 * 16 + 16)
                if past(unit, RING):
                    act.wait_ge(unit_mm, unit - RING + 1)
                act.activation(w_hi[:, r, :], w_raw[:, r, :], ACT.Copy).then_inc(w_hi_done, 1)

            for n in range(B - XR, B + 1):
                conv_step(n, n // XR, n % XR)
                if n == B - 1:
                    split_w(0, 0, 0)
                for s in H_EARLY.get(n, ()):
                    split_h(0, s)
            split_w(1, 0, 1)
            split_w(2, 0, 2)

            def group(g, first=False, last=False):
                for u in range(UNITS):
                    m = u - 1
                    if 0 <= m < KC:
                        if first and m == 0:
                            act.wait_ge(stat_saved, B)
                        if m == 0:
                            act.wait_ge(traits_now, g + 1)
                        act.wait_ge(unit_mm, g * UNITS + u)
                        if past(g, 1) or m >= 2:
                            act.wait_ge(act_done, g * KC + m - 1)
                        n, par = size(g) * C, m % 2
                        ps = bank[L1_BANK + par][:, 0:n]
                        act.activation(zz[:, par, 0:n], ps, ACT.Identity, scale=now[:, 2:3], bias=now[:, 4 + KC + m:5 + KC + m])
                        act.activation(th[:, par, 0:n], ps, ACT.Tanh, scale=now[:, 3:4], bias=now[:, 4 + 2 * KC + m:5 + 2 * KC + m]).then_inc(two_done, 1)
                        act.activation(ge[:, par, 0:n], ps, ACT.Gelu, bias=now[:, 4 + m:5 + m]).then_inc(funcs_done, 1)
                    if not (last and u + 3 >= UNITS):
                        split_w(g * UNITS + u + 3, g * 4 + (u + 3) // 4, (u + 3) % 4)
                    if 0 <= m < KC:
                        act.wait_ge(act_done, g * KC + m + 1)
                        act.activation(act_hi[:, m, 0:n], act_f[:, par, 0:n], ACT.Copy).then_inc(act_hi_done, 1)
                    if not last:
                        for s in range(*(H_STEPS_0 if first else H_STEPS).get(u, (0, 0))):
                            if s == 0:
                                act.wait_ge(unit_mm, g * UNITS + KC)
                            if s < size(g + 1):
                                split_h(g + 1, s)
                    if first and u == 4:
                        act.wait_ge(pick_in, 2)
                        for e in range(E):
                            score_out = act.activation(route[0:B, C * e:C * e + C], bank[4][0:B, C * e:C * e + C], ACT.Identity,
                                                       bias=route[0:B, 388 + e:389 + e])
                        score_out.then_inc(scores_in, 1)
                    if first and u == 13:
                        act.wait_ge(hot_mm, 1)
                        cw = bank[7][:, 0:NSLOT].rearrange("p (t h) -> p t h", h=2)
                        for h in range(2):
                            kept = act.activation(coefs[C * h:C * h + C, :], cw[C * h:C * h + C, :, h], ACT.Copy)
                        kept.then_inc(routed, 1)
                    if first and u == 8:
                        act.wait_ge(exp_in, 1)
                        act.activation(route[0:B, 192:384], route[0:B, 0:192], ACT.Exp).then_inc(exp_done, 1)

            group(0, first=True)
            with act.Fori(1, SIXES - 1) as g:
                group(g)
            for g in range(SIXES - 1, GROUPS):
                group(g, last=g == GROUPS - 1)
            rows_last = [act.value_load(table[0:1, NSLOT - FEW + t:NSLOT - FEW + t + 1], min_val=0, max_val=ROWS - 1) for t in range(2, FEW)]
            act.wait_ge(acc_done, 2 * tiles_before(GROUPS))
            for t, at in zip(range(2, FEW), rows_last):
                act.dma_start(out[ds(at, 1), :, 512:D].rearrange("b c l -> (b c) l"),
                              acc[C * (t % 2):C * (t % 2) + C, t // 2, 512:D]).then_inc(last_out, 16)

        @block.vector
        def _(dve):
            step = [0]

            def link(ins):
                step[0] += 1
                ins.then_inc(dve_step, 1)
                dve.wait_ge(dve_step, step[0])

            dve.memset(w_blocks[0:C, K:K + 1, :], 0.0)
            dve.memset(w_blocks[C:P, 0:1, :], 0.0)
            dve.wait_ge(s_wn, 32)
            dve.wait_ge(of_group_done, 1)
            for q in range(2):
                half = slice(q * C, (q + 1) * C)
                for g in range(C // CG):
                    col = q * (C // CG) + g
                    last = dve.tensor_scalar(w_blocks[half, q:q + K, g * CG:(g + 1) * CG], w_nat[half].rearrange("o c k -> o k c"),
                                             of_group[half, col:col + 1], None, ALU.mult)
            last.then_inc(blocks_done, 1)
            dve.wait_ge(blocks_tr, 1)
            dve.tensor_copy(t_hi[:, 0:4, :], bank[4][:, :].rearrange("p (d m) -> p d m", m=P))
            link(dve.tensor_copy(t_hi[:, 4, :], bank[5][:, 0:P]))
            dve.tensor_tensor(t_lo[:, 0:4, :], bank[4][:, :].rearrange("p (d m) -> p d m", m=P), t_hi[:, 0:4, :].bitcast(f32), ALU.subtract)
            dve.tensor_tensor(t_lo[:, 4, :], bank[5][:, 0:P], t_hi[:, 4, :].bitcast(f32), ALU.subtract)
            dve.wait_ge(pad_zero, 2)

            def split_x(n, j):
                dve.wait_ge(x_hi_done, n + 1)
                dve.tensor_tensor(x_lo[:, j % 2, 2:2 + J], x_raw[:, j, 0:L:2], x_hi[:, j % 2, 2:2 + J].bitcast(f32),
                                  ALU.subtract).then_inc(x_lo_done, 1)

            def conv_step(n, it, j):
                par = (j + 1) % 2
                if past(n, 2):
                    dve.wait_ge(tr_mm, n - 1)
                    if past(n, 4):
                        dve.wait_ge(h_out[j % 2], it * 32 + (j - 2) // 2 * 16)
                    dve.tensor_copy(ht[:, j % 2, :], bank[2 + j % 2][:, :]).then_inc(ht_done, 1)
                if not (isinstance(n, int) and n + 1 >= B):
                    split_x(n + 1, (j + 1) % XR)
                if past(n, 1) and not (isinstance(n, int) and n > B):
                    dve.wait_ge(conv_done, n)
                    if not past(n, 2):
                        dve.wait_ge(gate_done, 1)
                    if past(n, 3):
                        dve.wait_ge(stat_saved, n - 2)
                    for e in range(E):
                        last = dve.tensor_tensor_reduce(out=junk_l[:, par, e, :], in0=conv[:, par, :], in1=gate[:, e, :], scale=1.0, scalar=0.0,
                                                        op0=ALU.mult, op1=ALU.add, accum_out=stat_now[:, par, e:e + 1])
                    last.then_inc(logit_done, 1)

            dve.wait_ge(small_tr, 1)
            dve.tensor_copy(c_t[:, :], bank[6][:, 0:B])
            dve.tensor_copy(cw_t[:, :], bank[6][:, P:2 * P]).then_inc(small_done, 1)
            split_x(0, 0)
            dve.wait_ge(ctx_mm, 1)
            dve.wait_ge(s_bias, 32)
            dve.tensor_scalar(shift[:, :], bank[7][:, 0:B], bias_col[:, 0:1], None, ALU.add).then_inc(shift_done, 1)
            r = lambda a, n, rows=B: route[0:rows, a:a + n]
            lge, exe = [r(64 * e, C) for e in range(E)], [r(192 + 64 * e, C) for e in range(E)]
            vis, txt, ratio = r(384, 1), r(385, 1), r(386, 1)
            add, score, best = r(388, E), r(391, E), r(394, 1)
            top, low, t0, t1 = r(400, C), r(464, C), r(528, C), r(592, C)
            v0, v1, rd = r(656, C), r(720, C), r(784, C)
            g10, g20, g21 = r(850, 1), r(851, 1), r(852, 1)
            wins, sel, first, second, rest_sel = r(856, E), r(SEL, E), r(864, E), r(868, E), r(REST, E)
            tot = r(880, E, P)
            rest = route[:, 1912:1912 + E * CUTS].rearrange("p (e c) -> p e c", e=E)
            less = route[:, 2480:2480 + E * CUTS * MOST].rearrange("p (e c k) -> p e c k", e=E, k=MOST)
            take = route[:, 3008:3008 + 2 * E * CUTS].rearrange("p (e c) -> p e c", c=CUTS)
            cost, pick, top_pick = r(1962, CUTS, P), r(1978, CUTS, P), r(1994, 1, P)
            fav, lead, is_top, their_slot = r(2020, E, P), r(2023, 1, P), r(2024, E, P), r(2027, 1)
            own = r(1996, 2 * E, P)
            ahead = r(2002, 2 * E, P)
            own2, ahead2 = (t.rearrange("p (a e) -> p a e", a=2) for t in (own, ahead))
            in_large, start, shift_few, few = r(2008, E), r(2011, E), r(2014, E), r(2017, E)
            slot = r(904, E)
            wt = [r(912 + P * e, P) for e in range(E)]
            hot = [r(HOT + NSLOT * e, NSLOT) for e in range(E)]
            rows = [r(ROW + NSLOT * e, NSLOT) for e in range(E)]
            ge0, ge1 = r(1720, GROUPS - 1, P), r(1750, GROUPS - 1, P)

            def choose(logits, n):
                b = slice(0, n)
                dve.reduce_sum(vis[b], logits[b, 192:192 + VIS], AX.X)
                link(dve.reduce_sum(txt[b], logits[b, 192 + VIS:256], AX.X))
                link(dve.tensor_scalar(vis[b], vis[b], 1.0 / (VIS * L), 1e-8, ALU.mult, ALU.add))
                link(dve.reciprocal(vis[b], vis[b]))
                link(dve.tensor_scalar(ratio[b], txt[b], 1.0 / ((C - VIS) * L), vis[b], ALU.mult, ALU.mult))
                link(dve.scalar_tensor_tensor(out=add[b], in0=gate_last[b, :], scalar=ratio[b], in1=gate_bias[b, :], op0=ALU.mult, op1=ALU.add))
                link(dve.tensor_tensor(score[b], logits[b, 0:192].rearrange("b (e s) -> b e s", e=E)[:, :, 0], add[b], ALU.add))
                link(dve.reduce_max(best[b], score[b], AX.X))
                link(dve.tensor_scalar(score[b], score[b], best[b], -87.3, ALU.subtract, ALU.max))
                d0, d1, d2 = (score[b, e:e + 1] for e in range(E))
                dve.tensor_tensor(g10[b], d1, d0, ALU.is_gt)
                dve.tensor_tensor(g20[b], d2, d0, ALU.is_gt)
                link(dve.tensor_tensor(g21[b], d2, d1, ALU.is_gt))
                dve.tensor_tensor(wins[b, 0:1], g10[b], g20[b], ALU.add)
                dve.tensor_tensor(wins[b, 1:2], g21[b], g10[b], ALU.subtract)
                link(dve.tensor_tensor(wins[b, 2:3], g20[b], g21[b], ALU.add))
                dve.tensor_scalar(sel[b, 0:1], wins[b, 0:1], 1.5, None, ALU.is_lt)
                dve.tensor_scalar(sel[b, 1:2], wins[b, 1:2], 0.5, None, ALU.is_lt)
                last = dve.tensor_scalar(sel[b, 2:3], wins[b, 2:3], 0.5, None, ALU.is_gt)
                if n < B:
                    last.then_inc(pick_in, 1)
                else:
                    link(last)

            def early_pairs():
                b = slice(0, EARLY)
                counts, ranks = bank[5][:, 0:E], bank[5][b, 8:8 + E]
                dve.wait_ge(pick_mm, 1)
                dve.scalar_tensor_tensor(out=early[b], in0=ranks, scalar=float(SLOTS), in1=sel[b], op0=ALU.is_lt, op1=ALU.mult)
                link(dve.tensor_copy(tot, counts))
                link(dve.reduce_max(lead, tot, AX.X))
                link(dve.tensor_scalar(is_top, tot, lead, None, ALU.is_equal))
                dve.tensor_copy(fav[:, 0:1], is_top[:, 0:1])
                dve.tensor_tensor(fav[:, 1:2], is_top[:, 1:2], is_top[:, 0:1], ALU.is_gt)
                link(dve.tensor_scalar(fav[:, 2:3], is_top[:, 1:2], is_top[:, 0:1], 0.5, ALU.max, ALU.is_lt))
                link(dve.tensor_tensor(early[b], early[b], fav[b], ALU.mult))
                link(dve.scalar_tensor_tensor(out=early_slot[b], in0=ranks, scalar=1.0, in1=early[b], op0=ALU.add, op1=ALU.mult))
                link(dve.reduce_sum(their_slot[b], early_slot[b], AX.X))
                dve.scalar_tensor_tensor(out=rows[0][b, 0:SLOTS], in0=slot_no[b, 0:SLOTS], scalar=their_slot[b], in1=rel[b, 0:SLOTS],
                                         op0=ALU.is_equal, op1=ALU.mult).then_inc(row_in, 1)

            def early_table():
                link(dve.tensor_scalar(lead, fav[:, 0:1], 0.5, None, ALU.is_lt))
                dve.tensor_tensor(table[0:1, NSLOT:NSLOT + 1], lead[0:1], fav[0:1, 2:3], ALU.add).then_inc(early_routed, 1)
                dve.wait_ge(row_mm, 1)
                dve.tensor_tensor(table[0:1, 0:SLOTS], bank[6][0:1, 0:SLOTS], spare[0:1, 0:SLOTS], ALU.add).then_inc(early_routed, 1)

            def choose_all():
                dve.wait_ge(fold_mm, 2)
                choose(bank[4], B)
                dve.tensor_tensor(rest_sel, sel, early[:, :], ALU.subtract).then_inc(pick_in, 1)
                dve.tensor_scalar(first[:, 0:1], wins[:, 0:1], 0.5, None, ALU.is_lt)
                dve.tensor_scalar(first[:, 1:2], wins[:, 1:2], -0.5, None, ALU.is_lt)
                dve.tensor_scalar(first[:, 2:3], wins[:, 2:3], 1.5, None, ALU.is_gt)

            def plan_groups():
                dve.wait_ge(pick_mm, 2)
                dve.memset(ahead2[:, :, 0:1], 0.0)
                link(dve.tensor_copy(tot, bank[5][:, 0:E]))
                wide = [P, E, CUTS]
                link(dve.tensor_tensor(rest, tot.unsqueeze(2).to_broadcast(wide), plan[:, E:2 * E, :], ALU.subtract))
                wide = [P, E * CUTS, MOST]
                link(dve.tensor_tensor(less.rearrange("p e c k -> p (e c) k"), steps[:, :].unsqueeze(1).to_broadcast(wide),
                                       rest.rearrange("p e c -> p (e c)").unsqueeze(2).to_broadcast(wide), ALU.is_lt))
                link(dve.reduce_sum(plan[:, 0:E, :], less, AX.X))
                link(dve.reduce_sum(cost, plan[:, 0:E, :].rearrange("p e c -> p c e"), AX.X))
                link(dve.scalar_tensor_tensor(out=pick, in0=cost, scalar=float(SIXES - 1), in1=rank[:, :], op0=ALU.is_le, op1=ALU.mult))
                link(dve.reduce_max(top_pick, pick, AX.X))
                link(dve.tensor_scalar(pick, pick, top_pick, None, ALU.is_equal))
                link(dve.tensor_tensor(take, plan[:, :, :], pick.unsqueeze(1).to_broadcast([P, 2 * E, CUTS]), ALU.mult))
                link(dve.reduce_sum(own, take, AX.X))
                dve.tensor_copy(ahead2[:, :, 1:2], own2[:, :, 0:1])
                link(dve.tensor_tensor(ahead2[:, :, 2:3], own2[:, :, 0:1], own2[:, :, 1:2], ALU.add))
                for a, part in enumerate((slice(0, SIXES - 1), slice(SIXES - 1, GROUPS - 1))):
                    dve.tensor_scalar(ge0[:, part], group_no[:, part], ahead[:, E * a + 1:E * a + 2], None, ALU.is_ge)
                    last = dve.tensor_scalar(ge1[:, part], group_no[:, part], ahead[:, E * a + 2:E * a + 3], None, ALU.is_ge)
                link(last)
                dve.tensor_tensor(table[0:1, NSLOT + 1:NSLOT + GROUPS], ge0[0:1, :], ge1[0:1, :], ALU.add).then_inc(routed, 1)

            def plan_slots():
                place = bank[5][0:B, 8:8 + E]
                dve.tensor_scalar(in_large, own[0:B, 0:E], float(SLOTS), None, ALU.mult)
                link(dve.tensor_scalar(start, ahead[0:B, 0:E], float(SLOTS), None, ALU.mult))
                dve.tensor_tensor(few, place, in_large, ALU.is_ge)
                dve.tensor_tensor(slot, place, start, ALU.add)
                link(dve.scalar_tensor_tensor(out=shift_few, in0=ahead[0:B, E:2 * E], scalar=float((SIXES - 1) * SLOTS), in1=in_large, op0=ALU.add, op1=ALU.subtract))
                link(dve.tensor_tensor(shift_few, shift_few, start, ALU.subtract))
                link(dve.tensor_tensor(few, few, shift_few, ALU.mult))
                link(dve.tensor_tensor(slot, slot, few, ALU.add))
                link(dve.scalar_tensor_tensor(out=slot, in0=slot, scalar=1.0 + SLOTS, in1=rest_sel, op0=ALU.add, op1=ALU.mult))
                link(dve.tensor_tensor(slot, slot, early_slot[:, :], ALU.add))
                for e in range(E):
                    last = dve.scalar_tensor_tensor(out=rows[e], in0=slot_no[:, :], scalar=slot[:, e:e + 1], in1=rel[:, :], op0=ALU.is_equal, op1=ALU.mult)
                last.then_inc(row_in, 1)
                for e in range(E):
                    dve.tensor_scalar(hot[e], slot_no[:, :], slot[:, e:e + 1], None, ALU.is_equal)

            def keep_rows():
                dve.wait_ge(row_mm, 2)
                dve.tensor_tensor(table[0:1, SLOTS:NSLOT], bank[5][0:1, 256 + SLOTS:256 + NSLOT], spare[0:1, SLOTS:NSLOT], ALU.add).then_inc(routed, 1)

            def below_top():
                dve.tensor_tensor(second, sel, first, ALU.subtract)
                dve.wait_ge(scores_in, 1)
                link(dve.tensor_tensor(top, lge[0], lge[1], ALU.max))
                link(dve.tensor_tensor(top, top, lge[2], ALU.max))
                for e in range(E):
                    last = dve.tensor_tensor(lge[e], lge[e], top, ALU.subtract)
                last.then_inc(exp_in, 1)

            def weigh():
                dve.wait_ge(exp_done, 1)
                link(dve.tensor_tensor(t0, exe[0], exe[1], ALU.add))
                link(dve.tensor_tensor(t0, t0, exe[2], ALU.add))
                link(dve.reciprocal(t0, t0))
                for e in range(E):
                    last = dve.tensor_tensor(exe[e], exe[e], t0, ALU.mult)
                link(last)
                dve.tensor_tensor(top, exe[0], exe[1], ALU.max)
                link(dve.tensor_tensor(low, exe[0], exe[1], ALU.min))
                dve.tensor_tensor(t1, top, exe[2], ALU.min)
                link(dve.tensor_tensor(v0, top, exe[2], ALU.max))
                link(dve.tensor_tensor(v1, low, t1, ALU.max))
                link(dve.scalar_tensor_tensor(out=rd, in0=v0, scalar=1e-8, in1=v1, op0=ALU.add, op1=ALU.add))
                link(dve.reciprocal(rd, rd))
                dve.tensor_tensor(v0, v0, rd, ALU.mult)
                link(dve.tensor_tensor(v1, v1, rd, ALU.mult))
                for e in range(E):
                    last = dve.tensor_scalar(exe[e], v0, first[:, e:e + 1], None, ALU.mult)
                link(last)
                for e in range(E):
                    for h in range(2):
                        last = dve.scalar_tensor_tensor(out=wt[e][:, C * h:C * h + C], in0=v1, scalar=second[:, e:e + 1], in1=exe[e],
                                                        op0=ALU.mult, op1=ALU.add)
                last.then_inc(hot_in, 1)

            for j in range(XR):
                conv_step(j, 0, j)
            dve.memset(early[:, :], 0.0)
            dve.memset(early_slot[:, :], 0.0)
            dve.wait_ge(b1_tr, 1)
            for e, trait in enumerate(((1.0, 0.0, 0.0, 1.0), (0.0, 1.0, 0.0, 1.0), (0.0, 0.0, 0.5, 0.5))):
                b1_e = bank[6][:, 2 * P + e * KC:2 * P + (e + 1) * KC]
                for k in range(4):
                    dve.memset(traits[:, e, k:k + 1], trait[k])
                dve.tensor_copy(traits[:, e, 4:4 + KC], b1_e)
                dve.tensor_scalar(traits[:, e, 4 + KC:4 + 2 * KC], b1_e, trait[2], None, ALU.mult)
                dve.tensor_scalar(traits[:, e, 4 + 2 * KC:4 + 3 * KC], b1_e, trait[3], None, ALU.mult)
            with dve.Fori(1, EARLY_AT) as it:
                for j in range(XR):
                    conv_step(it * XR + j, it, j)
            for j in range(XR):
                conv_step(EARLY_AT * XR + j, EARLY_AT, j)
                if j == 0:
                    dve.wait_ge(fold_mm, 1)
                    dve.wait_ge(s_gl, 32)
                    dve.wait_ge(consts, 1)
                    choose(bank[6], EARLY)
                if j == 2:
                    early_pairs()
            early_table()
            with dve.Fori(EARLY_AT + 1, B // XR - 1) as it:
                for j in range(XR):
                    conv_step(it * XR + j, it, j)

            def split_h(g, s):
                dve.wait_ge(h_hi_done, slots_before(g) + s + 1)
                dve.tensor_tensor(h_lo[:, s, :], h_raw[:, s, :], h_hi[:, s, :].bitcast(f32), ALU.subtract).then_inc(h_lo_done, 1)

            def split_w(unit, r):
                dve.wait_ge(w_hi_done, unit + 1)
                dve.tensor_tensor(w_lo[:, r, :], w_raw[:, r, :], w_hi[:, r, :].bitcast(f32), ALU.subtract).then_inc(w_lo_done, 1)

            for n in range(B - XR, B + 2):
                conv_step(n, n // XR, n % XR)
                for s in H_EARLY.get(n, ()):
                    split_h(0, s)
                if n == B - 1:
                    split_w(0, 0)
            dve.wait_ge(w_lo_done, 2)
            split_w(2, 2)

            B2_STEPS, B2_STEPS_0 = {8: (0,), 9: (1,), 10: (2,)}, {14: (0,), 15: (1, 2)}
            def finish(g, half):
                for t in range(size(g) // 2):
                    dst = acc[:, t, half * 512:(half + 1) * 512]
                    dve.scalar_tensor_tensor(out=dst, in0=bank[TT * half + t][:, :], scalar=coef_now[:, t:t + 1], in1=dst,
                                             op0=ALU.mult, op1=ALU.add).then_inc(acc_done, 1)

            def group(g, first=False, last=False):
                e = dve.value_load(table[0:1, ds(g + NSLOT, 1)], min_val=0, max_val=E - 1)
                for u in range(UNITS):
                    m, n = u - 1, size(g) * C
                    if u == 0 and past(g, 1):
                        dve.wait_ge(unit_mm, g * UNITS)
                        finish(g - 1, 1)
                    if 0 <= m < KC:
                        par = m % 2
                        if m == 0:
                            dve.wait_ge(traits_now, g + 1)
                        dve.wait_ge(two_done, g * KC + m + 1)
                        if past(g, 1) or m >= 2:
                            dve.wait_ge(act_hi_done, g * KC + m - 1)
                            if first:
                                dve.wait_ge(act_lo_done, m - 1)
                        step_a = dve.scalar_tensor_tensor(out=mix[:, par, 0, 0:n], in0=zz[:, par, 0:n], scalar=now[:, 0:1], in1=th[:, par, 0:n],
                                                          op0=ALU.add, op1=ALU.mult)
                        step_a.then_inc(mixed, 1)
                        dve.wait_ge(mixed, g * 16 + 2 * m + 1)
                        dve.tensor_tensor(mix[:, par, 1, 0:n], mix[:, par, 0, 0:n], zz[:, par, 0:n], ALU.add).then_inc(mixed, 1)
                        dve.wait_ge(mixed, g * 16 + 2 * m + 2)
                        dve.wait_ge(funcs_done, g * KC + m + 1)
                        dve.scalar_tensor_tensor(out=act_f[:, par, 0:n], in0=ge[:, par, 0:n], scalar=now[:, 1:2], in1=mix[:, par, 1, 0:n],
                                                 op0=ALU.mult, op1=ALU.add).then_inc(act_done, 1)
                    if first and u + 2 in POOL_UNITS:
                        dve.wait_ge(w_lo_done, u + 3)
                    if not (last and u + 3 >= UNITS or first and u + 3 in POOL_UNITS):
                        split_w(g * UNITS + u + 3, (u + 3) % 4)
                    if 0 <= m < KC and not first:
                        dve.wait_ge(act_hi_done, g * KC + m + 1)
                        dve.tensor_tensor(act_lo[:, m, 0:n], act_f[:, par, 0:n], act_hi[:, m, 0:n].bitcast(f32), ALU.subtract).then_inc(act_lo_done, 1)
                    if first and u == 2:
                        choose_all()
                    if first and u == 5:
                        plan_groups()
                    if first and u == 6:
                        plan_slots()
                        below_top()
                    if first and u == 9:
                        keep_rows()
                        weigh()
                    if not last:
                        for s in range(*(H_STEPS_0 if first else H_STEPS).get(u, (0, 0))):
                            if s < size(g + 1) and not (first and s % 2 == 1):
                                split_h(g + 1, s)
                    for t in (B2_STEPS_0 if first else B2_STEPS).get(u, ()):
                        if t < size(g) // 2:
                            if t == 0:
                                dve.wait_ge(acc_in, slots_before(g + 1) * 16)
                                dve.wait_ge(coef_ready, g + 1)
                                dve.wait_ge(s_b2, 48)
                            dve.scalar_tensor_tensor(out=acc[:, t, :], in0=b2_all[:, ds(e, 1), :].rearrange("p e d -> p (e d)"),
                                                     scalar=coef_now[:, t:t + 1], in1=acc[:, t, :], op0=ALU.mult, op1=ALU.add).then_inc(acc_b2, 1)
                    if u == (15 if first else 12):
                        dve.wait_ge(unit_mm, g * UNITS + 12)
                        dve.wait_ge(acc_b2, tiles_before(g + 1))
                        finish(g, 0)

            group(0, first=True)
            with dve.Fori(1, SIXES - 1) as g:
                group(g)
            for g in range(SIXES - 1, GROUPS):
                group(g, last=g == GROUPS - 1)
            dve.wait_ge(unit_mm, GROUPS * UNITS)
            finish(GROUPS - 1, 1)

        @block.tensor
        def _(pe):
            pe.wait_ge(ident_done, 1)
            pe.wait_ge(blocks_done, 1)
            for d in range(TAPS2):
                last = pe.transpose(bank[4][:, d * P:(d + 1) * P] if d < 4 else bank[5][:, 0:P],
                                    w_blocks[:, 2 * d:2 * d + 2, :].rearrange("m p c -> m (p c)"), ident[:, :])
            last.then_inc(blocks_tr, 1)
            pe.wait_ge(s_c, 16)
            pe.transpose(bank[6][:, 0:B], c_nat[:, :], ident[0:B, 0:B])
            pe.wait_ge(s_cw, 32)
            pe.transpose(bank[6][:, P:2 * P], cw_nat[:, :], ident[:, :]).then_inc(small_tr, 1)
            pe.wait_ge(small_done, 1)
            pe.matmul(bank[7][:, 0:B], cw_t[:, :], c_t[:, :], start=True, stop=True).then_inc(ctx_mm, 1)

            def conv_step(n, j):
                if j is not None:
                    par = j % 2
                    pe.wait_ge(x_lo_done, n + 1)
                    if past(n, 2):
                        pe.wait_ge(conv_done, n - 1)
                    for d in range(TAPS2):
                        for i, (a, b) in enumerate(((t_hi, x_hi), (t_hi, x_lo), (t_lo, x_hi))):
                            last = pe.matmul(bank[par][:, :], a[:, d, :], b[:, par, d:d + J],
                                             start=(d + i == 0), stop=(d == TAPS2 - 1 and i == 2))
                    last.then_inc(conv_mm, 1)
                if past(n, 1):
                    par = ((j or 0) + 1) % 2
                    pe.wait_ge(conv_done, n)
                    if past(n, 3):
                        pe.wait_ge(ht_done, n - 2)
                    for k in range(4):
                        last = pe.transpose(bank[2 + par][:, k * P:(k + 1) * P], conv[:, par, k * P:(k + 1) * P], ident[:, :])
                    last.then_inc(tr_mm, 1)

            def sums(to, n):
                for e in range(4):
                    last = pe.matmul(to[0:n, 64 * e:64 * e + 64], stat[:, 0:n, e], fold[:, :], start=True, stop=True)
                last.then_inc(fold_mm, 1)

            def count(pairs, n):
                pe.matmul(bank[5][:, 0:E], ones[0:n, :], route[0:n, pairs:pairs + E], start=True, stop=True)
                pe.matmul(bank[5][0:n, 8:8 + E], before[0:n, 0:n], route[0:n, pairs:pairs + E], start=True, stop=True).then_inc(pick_mm, 1)

            for j in range(4):
                conv_step(j, j)
            pe.wait_ge(s_b1, 16)
            pe.transpose(bank[6][:, 2 * P:2 * P + E * KC], b1_nat[:, :], ident[0:E * KC, 0:E * KC]).then_inc(b1_tr, 1)
            with pe.Fori(1, EARLY_AT) as it:
                for j in range(4):
                    conv_step(it * 4 + j, j)
            for j in range(4):
                if j == 0:
                    pe.wait_ge(consts, 1)
                    pe.wait_ge(stat_saved, EARLY)
                    sums(bank[6], EARLY)
                if j == 2:
                    pe.wait_ge(pick_in, 1)
                    count(SEL, EARLY)
                conv_step(EARLY_AT * 4 + j, j)
            pe.wait_ge(row_in, 1)
            pe.matmul(bank[6][:, 0:SLOTS], ones[0:EARLY, :], route[0:EARLY, ROW:ROW + SLOTS], start=True, stop=True).then_inc(row_mm, 1)
            with pe.Fori(EARLY_AT + 1, B // 4) as it:
                for j in range(4):
                    conv_step(it * 4 + j, j)
            conv_step(B, None)

            def weigh():
                pe.wait_ge(hot_in, 1)
                for e in range(E):
                    last = pe.matmul(bank[7][:, 0:NSLOT], route[0:B, 912 + P * e:912 + P * (e + 1)],
                                     route[0:B, HOT + NSLOT * e:HOT + NSLOT * (e + 1)], start=(e == 0), stop=(e == E - 1))
                last.then_inc(hot_mm, 1)

            def group(g, first=False):
                for u in range(UNITS):
                    if first and u == 1:
                        pe.wait_ge(stat_saved, B)
                        sums(bank[4], B)
                    if first and u == 5:
                        pe.wait_ge(pick_in, 2)
                        count(REST, B)
                    if first and u == 9:
                        pe.wait_ge(row_in, 2)
                        for e in range(E):
                            at = ROW + NSLOT * e
                            last = pe.matmul(bank[5][:, 256:256 + NSLOT], ones[:, :], route[0:B, at:at + NSLOT], start=(e == 0), stop=(e == E - 1))
                        last.then_inc(row_mm, 1)
                    if first and u == 13:
                        weigh()
                    if first and u == 12:
                        pe.wait_ge(routed, 2)
                        pe.wait_ge(scores_in, 1)
                    if first and u == 15:
                        pe.wait_ge(routed, 3)
                    pe.wait_ge(w_lo_done, g * UNITS + u + 1)
                    if u < KC:
                        if u == 0:
                            pe.wait_ge(h_lo_done, slots_before(g + 1))
                        if past(g, 1) or u >= 2:
                            pe.wait_ge(funcs_done, g * KC + u - 1)
                        w = u % RING
                        for k in range(KC):
                            for i, (a, b) in enumerate(((w_hi, h_hi), (w_hi, h_lo), (w_lo, h_hi))):
                                last = pe.matmul(bank[L1_BANK + u % 2][:, 0:size(g) * C], a[:, w, k * P:(k + 1) * P], b[:, 0:size(g), k * C:(k + 1) * C],
                                                 start=(k + i == 0), stop=(k == KC - 1 and i == 2))
                    else:
                        half, pair, w = (u - 8) // 4, (u - 8) % 4, u % RING
                        if u in (8, 12) and past(g, 1):
                            pe.wait_ge(acc_done, tiles_before(g - 1 + half) + tiles_before(g))
                        if half == 0:
                            pe.wait_ge(act_lo_done, g * KC + 2 * pair + 2)
                        for f in range(2):
                            k = 2 * pair + f
                            for t in range(size(g) // 2):
                                for i, (a, b) in enumerate(((act_hi, w_hi), (act_hi, w_lo), (act_lo, w_hi))):
                                    last = pe.matmul(bank[TT * half + t][:, :], a[:, k, t * P:(t + 1) * P], b[:, w, f * 512:(f + 1) * 512],
                                                     start=(k + i == 0), stop=(k == KC - 1 and i == 2))
                    last.then_inc(unit_mm, 1)

            group(0, first=True)
            with pe.Fori(1, SIXES) as g:
                group(g)
            for g in range(SIXES, GROUPS):
                group(g)


_INS = ["x", "cond_128", "fside_S_0", "L0_cond_weight", "L0_cond_c_weight", "L0_ffn_gate_w", "L0_ffn_gate_b",
        "L0_ffn_w1", "L0_ffn_b1", "L0_ffn_w2", "L0_ffn_b2"]


def kernel(**inputs):
    import numpy as _np
    import concourse.bacc as _bacc
    from concourse import mybir as _mybir
    from concourse.bass_utils import run_bass_kernel_spmd as _run

    nc = _bacc.Bacc("TRN2", target_bir_lowering=False, num_devices=1)
    arrays, args = {}, []
    for name in _INS:
        a = _np.ascontiguousarray(inputs[name])
        arrays[f"in_{name}_dram"] = a
        args.append(nc.dram_tensor(f"in_{name}_dram", a.shape, _mybir.dt.from_np(a.dtype), kind="ExternalInput").ap())
    args.append(nc.dram_tensor("out_0_dram", (ROWS, C, L), _mybir.dt.float32, kind="ExternalOutput").ap())
    build(nc, *args)
    r = _run(nc, [arrays], core_ids=[0])
    return r.results[0]["out_0_dram"][:B]
```
